# Optimizing a Trainium2 kernel written in Bass

```python
import numpy as np
import jax
import jax.numpy as jnp

def _softmax(x, axis=-1):
    return jax.nn.softmax(x, axis=axis)
def _gelu(x):
    return jax.nn.gelu(x, approximate=True)
def _silu(x):
    return jax.nn.silu(x)
def _sigmoid(x):
    return jax.nn.sigmoid(x)
def _layernorm(x, axis=-1, eps=1e-5):
    m = jnp.mean(x, axis=axis, keepdims=True)
    v = jnp.var(x, axis=axis, keepdims=True)
    return (x - m) / jnp.sqrt(v + eps)
def _scatter_add(tgt, idx, src, axis=0):
    return tgt.at[idx].add(src)
def _segment_sum(src, seg, n):
    return jax.ops.segment_sum(src, seg, n)

kernel_name = 'mk_adj_preln_d2_adj_128_4a6bc6'

def setup_inputs(seed: int = 0):
    np.random.seed(seed)
    _w = jnp.asarray
    def _rec_inputs():
        import jax
        import jax.numpy as jnp
        _gk = jax.random.key(seed)
        x = -0.000929 + 1 * jax.random.normal(jax.random.fold_in(_gk, 1), (8192, 128), jnp.float32)
        _a = jax.random.bernoulli(jax.random.fold_in(_gk, 2), 0.000976562, (8192, 8192))
        _a = jnp.logical_or(_a, jnp.swapaxes(_a, -1, -2))
        _a = jnp.logical_or(_a, jnp.eye(8192, dtype=bool))
        _af = _a.astype(jnp.float32)
        _af = _af * jax.random.uniform(jax.random.fold_in(_gk, 3), (8192, 8192), jnp.float32, 0.05, 0.0598829)
        adj = _af
        return x, adj
    x, adj = _rec_inputs()
    def _L0_gnn_setup():
        import jax, jax.numpy as jnp
        import numpy as np
        V0, V1, C = (64, 128, 128)
        V = V0 * V1
        key = jax.random.key(seed)
        ks = jax.random.split(key, 8)
        x = jax.random.normal(ks[0], (V, C), dtype=jnp.float32)
        edge_index = jax.random.randint(ks[1], (2, 100), 0, V)
        L = jnp.zeros((2, 2), dtype=jnp.float32)
        mass = jax.random.uniform(ks[2], (V,), dtype=jnp.float32) + 0.5
        evals0 = jax.random.uniform(ks[3], (V0,), dtype=jnp.float32) * 2.0
        evals1 = jax.random.uniform(ks[4], (V1,), dtype=jnp.float32) * 2.0
        evecs = jax.random.normal(ks[5], (V, V), dtype=jnp.float32) / np.float32(np.sqrt(V))
        diffusion_time = jax.random.uniform(ks[6], (2, C), dtype=jnp.float32)
        return {'x': x, 'edge_index': edge_index, 'L': L, 'mass': mass, 'evals0': evals0, 'evals1': evals1, 'evecs': evecs, 'diffusion_time': diffusion_time}
    _L0_gnn_all = _L0_gnn_setup()
    _L0_gnn_in = {k: v for k, v in _L0_gnn_all.items() if k in ('edge_index', 'L', 'mass', 'evals0', 'evals1', 'diffusion_time', )}
    del _L0_gnn_all

    def _L1_gnn_setup():
        import jax, jax.numpy as jnp
        import numpy as np
        N = 8192
        F_IN = 128
        F_OUT = 128
        BLOCK = 64

        def _graph_pool(out, adj):
            neg = jnp.asarray(jnp.finfo(out.dtype).min, out.dtype)

            def body(_, adj_blk):
                masked = jnp.where(adj_blk[:, :, None] != 0, out[None, :, :], neg)
                return (None, jnp.max(masked, axis=1))
            _, blocks = jax.lax.scan(body, None, adj.reshape(N // BLOCK, BLOCK, N))
            return blocks.reshape(N, out.shape[-1])
        key = jax.random.key(seed)
        k_in, k_adj, k_w, k_b = jax.random.split(key, 4)
        x = jax.random.normal(k_in, (N, F_IN), dtype=jnp.float32)
        adj = (jax.random.uniform(k_adj, (N, N)) < 0.01).astype(jnp.float32)
        adj = adj.at[jnp.arange(N), jnp.arange(N)].set(1.0)
        stdv = 1.0 / np.sqrt(F_OUT)
        weight = jax.random.uniform(k_w, (F_IN, F_OUT), minval=-stdv, maxval=stdv, dtype=jnp.float32)
        bias = jax.random.uniform(k_b, (F_OUT,), minval=-stdv, maxval=stdv, dtype=jnp.float32)
        return {'input': x, 'adj': adj, 'weight': weight, 'bias': bias}
    _L1_gnn_all = _L1_gnn_setup()
    _L1_gnn_in = {k: v for k, v in _L1_gnn_all.items() if k in ('weight', 'bias', )}
    del _L1_gnn_all

    return {
        "x": x,
        "adj": adj,
        "L0_gnn_edge_index": _L0_gnn_in["edge_index"],
        "L0_gnn_L": _L0_gnn_in["L"],
        "L0_gnn_mass": _L0_gnn_in["mass"],
        "L0_gnn_evals0": _L0_gnn_in["evals0"],
        "L0_gnn_evals1": _L0_gnn_in["evals1"],
        "L0_gnn_diffusion_time": _L0_gnn_in["diffusion_time"],
        "L1_gnn_weight": _L1_gnn_in["weight"],
        "L1_gnn_bias": _L1_gnn_in["bias"],
    }

def reference(x, adj, L0_gnn_edge_index, L0_gnn_L, L0_gnn_mass, L0_gnn_evals0, L0_gnn_evals1, L0_gnn_diffusion_time, L1_gnn_weight, L1_gnn_bias):
    import jax
    import jax.numpy as jnp
    def _L0_gnn_ref(x, edge_index, L, mass, evals0, evals1, evecs, diffusion_time):
        import jax, jax.numpy as jnp
        import numpy as np
        V0, V1, C = (64, 128, 128)
        V = V0 * V1
        x_spec = evecs.T @ (x * mass[:, None])
        e0 = jnp.exp(-evals0[:, None] * diffusion_time[0][None, :])
        e1 = jnp.exp(-evals1[:, None] * diffusion_time[1][None, :])
        diffusion_coefs = (e0[:, None, :] * e1[None, :, :]).reshape(V0 * V1, C)
        x_diffuse = evecs @ (diffusion_coefs * x_spec)
        return x_diffuse

    def _L1_gnn_ref(input, adj, weight, bias):
        import jax, jax.numpy as jnp
        import numpy as np
        N = 8192
        F_IN = 128
        F_OUT = 128
        BLOCK = 64

        def _graph_pool(out, adj):
            neg = jnp.asarray(jnp.finfo(out.dtype).min, out.dtype)

            def body(_, adj_blk):
                masked = jnp.where(adj_blk[:, :, None] != 0, out[None, :, :], neg)
                return (None, jnp.max(masked, axis=1))
            _, blocks = jax.lax.scan(body, None, adj.reshape(N // BLOCK, BLOCK, N))
            return blocks.reshape(N, out.shape[-1])
        h = input @ weight
        out = jnp.maximum(adj @ h + bias, 0.0)
        return _graph_pool(out, adj)

    h = jnp.maximum(_layernorm(x, axis=-1), 0.0)
    x = x + _L0_gnn_ref(h, L0_gnn_edge_index, L0_gnn_L, L0_gnn_mass, L0_gnn_evals0, L0_gnn_evals1, adj, L0_gnn_diffusion_time)
    h = jnp.maximum(_layernorm(x, axis=-1), 0.0)
    x = x + _L1_gnn_ref(h, adj, L1_gnn_weight, L1_gnn_bias)
    return x


_drawn_inputs = setup_inputs


def setup_inputs(seed=0):
    import zlib

    import numpy as np

    out = dict(_drawn_inputs(seed))
    spreads = {'L0_gnn_L': (0.0, 0.1)}
    factors = {'L0_gnn_mass': 26.604,
     'L0_gnn_evals0': 4.372,
     'L0_gnn_evals1': 4.808,
     'L1_gnn_bias': 3.091}
    for name, (base, spread) in spreads.items():
        noise = np.random.default_rng([zlib.crc32(name.encode()), seed]).standard_normal(out[name].shape)
        drawn = base * np.exp(spread * noise) if base else spread * noise
        out[name] = jnp.asarray(drawn.astype(out[name].dtype))
    for name, factor in factors.items():
        out[name] = (out[name] * factor).astype(out[name].dtype)
    return out
```

```python
from contextlib import ExitStack

import numpy as np

import concourse.bass as bass
from concourse import mybir

P = 128
W = 512
SEG = 256
TOP = 8
PARTS = 4
KQ = 24
ROWID, DEGREE, RANK, LIST = 24, 25, 26, 32
NB = 4
RT = 4
CH = 1024
LAG = 2
BIG = float(np.finfo(np.float32).max)
EPS = 1e-5

ALU = mybir.AluOpType
ACT = mybir.ActivationFunctionType
AX_X = mybir.AxisListType.X
F32 = mybir.dt.float32
BF16 = mybir.dt.bfloat16
U16 = mybir.dt.uint16
U32 = mybir.dt.uint32
I32 = mybir.dt.int32


class Steps:

    def __init__(self, sem, wait):
        self.sem, self.wait, self.base, self.n = sem, wait, 0, 0

    def step(self, ins):
        ins.then_inc(self.sem, 1)
        self.n += 1

    def settle(self):
        self.wait(self.sem, self.base + self.n)

    def enter(self, i, per):
        self.outer, self.per = self.base + self.n, per
        self.base, self.n = i * per + self.outer, 0

    def leave(self, rounds):
        assert self.n == self.per, (self.n, self.per)
        self.base, self.n = self.outer + rounds * self.per, 0


def diffusion_and_pool_kernel(nc, x, adj, mass, evals0, evals1, times, weight, bias, out):
    N, C = x.shape
    V0, V1 = evals0.shape[0], evals1.shape[0]
    assert C == P and V1 == P and V0 * V1 == N and adj.shape == (N, N)
    TILES = N // P
    HALF = N // 2
    BANKS = HALF // W
    HSEGS = HALF // SEG
    QC = HSEGS * TOP // 2
    BLOCKS = TILES // NB
    GROUPS = TILES // RT
    CHUNKS = N // CH
    JT = CH // P
    CSEGS = CH // SEG
    LT = NB // 2
    assert RT == NB == 2 * LT and CHUNKS % NB == 0 and BANKS <= 8
    DEG = KQ + 1
    OT = GROUPS // PARTS

    with ExitStack() as ctx:
        def sb(name, shape, dt=F32):
            return ctx.enter_context(nc.sbuf_tensor(name, shape, dt))

        def sem(name):
            return ctx.enter_context(nc.semaphore(name))

        def sems(name, n):
            return [sem(f"{name}{i}") for i in range(n)]

        out_table = [nc.dram_tensor(f"out_table{q}", [N // PARTS + 1, C], F32).ap() for q in range(PARTS)]
        sorted_lists = nc.dram_tensor("sorted_lists", [PARTS * N, LIST], U32).ap()
        pooled = nc.dram_tensor("pooled", [PARTS * N, C], F32).ap()
        x1_rows = nc.dram_tensor("x1_rows", [N, C], F32).ap()

        a_buf = sb("a_buf", [P, NB, RT * CH])
        h_rows = sb("h_rows", [P, TILES, C])
        y_buf = sb("y_buf", [P, N])
        lists = sb("lists", [P, TILES, PARTS, LIST], U16)
        at_buf = sb("at_buf", [P, 4, W])
        acc_s = sb("acc_s", [P, W])
        out_t = sb("out_t", [P, W])
        out_rows = sb("out_rows", [P, RT, C])
        work = sb("work", [P, max(3 * RT * C, DEG * TILES)])
        x_grp, x1_grp, xc = (work[:, i * RT * C:(i + 1) * RT * C].rearrange("p (r c) -> p r c", c=C) for i in range(3))
        z_buf = sb("z_buf", [P, 26 * 1024 // 4])
        ident = sb("ident", [P, P])
        w_sb = sb("w_sb", [P, C])
        cols_in = sb("cols_in", [3, P])
        cols = sb("cols", [P, 4])
        mass_in = sb("mass_in", [TILES, P])
        mass_c = sb("mass_c", [P, TILES])
        ev0 = sb("ev0_s", [P, V0])
        ev1 = sb("ev1_s", [P, V1])
        e0 = sb("e0", [P, V0])
        e1 = sb("e1", [P, V1])
        stats = sb("stats", [P, RT, 6])
        mv = sb("mv", [P, RT, 2])
        var = sb("var", [P, RT])
        rstd = sb("rstd", [P, RT])
        half_pow = sb("half_pow", [P, RT])
        ovf = sb("ovf", [P, TILES, 2])
        tri = sb("tri", [P, P], BF16)
        ones = sb("ones", [P, P], BF16)
        flag_c = sb("flag_c", [P, 4])
        flag_b = sb("flag_b", [P, 2], BF16)
        flag_i = sb("flag_i", [1, 2], I32)

        x_in = y_buf.rearrange("p (t c) -> p t c", c=C)
        y_t = y_buf
        sorted_s = y_buf[:, 0:PARTS * TILES * LIST].bitcast(U32).rearrange("p (u l) -> p u l", l=LIST)

        def carve(at, shape, dt):
            n = int(np.prod(shape)) * (2 if dt in (BF16, U16) else 4)
            v = z_buf[:, at // 4:(at + n) // 4]
            if dt != F32:
                v = v.bitcast(dt)
            names = "abcd"[:len(shape)]
            if len(shape) > 1:
                v = v.rearrange(f"p ({' '.join(names)}) -> p {' '.join(names)}", **dict(zip(names, shape)))
            return v, at + n

        key, z = carve(0, (LT * CH * 2 // SEG, SEG), BF16)
        iota_seg, z = carve(z, (SEG,), F32)
        seg_base, z = carve(z, (HSEGS * TOP,), F32)
        cand, z = carve(z, (LT, HSEGS, TOP), BF16)
        moved, z = carve(z, (LT, HSEGS * TOP), F32)
        keys0, z = carve(z, (LT, HSEGS * TOP), F32)
        keys1, z = carve(z, (LT, HSEGS * TOP), F32)
        keys2, z = carve(z, (LT, HSEGS * TOP), F32)
        raw, z = carve(z, (LT, 2, KQ), F32)
        fill, z = carve(z, (LT, 2, KQ), F32)
        assert z <= 26 * 1024
        onehot, z = carve(0, (PARTS * DEG, TILES), BF16)
        before, z = carve(z, (PARTS * DEG, TILES), BF16)
        gathered_rows, _ = carve(0, (2, KQ, C), F32)
        rank_n = work[:, 0:DEG * TILES]
        differs = rank_n[:, 0:TILES * (KQ - 1)]
        degree = sb("degree", [P, PARTS, TILES])
        deg_iota = sb("deg_iota", [P, PARTS, DEG])
        row_iota = sb("row_iota", [P, TILES])
        count = sb("count", [P, PARTS * DEG])
        count_b = sb("count_b", [P, PARTS * DEG], BF16)
        offs = sb("offs", [P, 3, PARTS * DEG])
        rank = sb("rank", [P, PARTS, TILES])
        scat = sb("scat", [P, 4, LIST], U32)
        glist = sb("glist", [P, 2, LIST], U32)
        grow = sb("grow", [P, 2, 2], U32)
        pool_acc = sb("pool_acc", [P, 2, C])
        none_row = sb("none_row", [1, C])

        ps = ctx.enter_context(nc.psum_tensor("ps", [P, 8, W], F32))
        TP, ACC, OUTB, ROWB, SMALL = 0, 4, 5, 6, 7

        consts = sem("consts")
        small_in = sem("small_in")
        x_first, x_rest = sem("x_first"), sem("x_rest")
        cols_turned, cols_copied, exp_done = sem("cols_turned"), sem("cols_copied"), sem("exp_done")
        a_loaded = sems("a_loaded", NB)
        pe_used, dve_used, dve_chunk = sem("pe_used"), sem("dve_used"), sem("dve_chunk")
        var_ready, rstd_ready = sem("var_ready"), sem("rstd_ready")
        xm_ready = sem("xm_ready")
        half_done, bank_read = sem("half_done"), sem("bank_read")
        yt_turned, y_ready = sem("yt_turned"), sem("y_ready")
        turned, at_copied, mm_done = sem("turned"), sem("at_copied"), sem("mm_done")
        acc_done, acc_saved = sem("acc_done"), sem("acc_saved")
        x_turned, x_turned_read = sem("x_turned"), sem("x_turned_read")
        xg_loaded, xg_read = sem("xg_loaded"), sem("xg_read")
        x1_ready, x1_stored, x1_free = sem("x1_ready"), sem("x1_stored"), sem("x1_free")
        h1_ready = sem("h1_ready")
        product_done, out_t_ready, rows_turned = sem("product_done"), sem("out_t_ready"), sem("rows_turned")
        rows_copied, out_stored = sem("rows_copied"), sem("out_stored")
        listed = sem("listed")
        counted, summed, ranked, flag_in, flag_sum, flag_set = (
            sem("counted"), sem("summed"), sem("ranked"), sem("flag_in"), sem("flag_sum"), sem("flag_set"))
        scat_staged, scat_done = sem("scat_staged"), sems("scat_done", 4)
        lists_sorted, lists_loaded = sem("lists_sorted"), sem("lists_loaded")
        glist_ready, acc_ready = sem("glist_ready"), sem("acc_ready")
        rows_in, acc_out = sems("rows_in", 2), sems("acc_out", 2)
        none_stored = sem("none_stored")
        pool_held, dve_held, act_held, sp_held = sem("pool_held"), sem("dve_held"), sem("act_held"), sem("sp_held")
        dve_step, epi_step, pool_step, red_step, fin_step = (
            sem("dve_step"), sem("epi_step"), sem("pool_step"), sem("red_step"), sem("fin_step"))
        fin_loaded, fin_stored, fin_ready = sems("fin_loaded", 2), sems("fin_stored", 2), sem("fin_ready")
        dense_a, dense_out, dense_x, dense_st = sem("dense_a"), sem("dense_out"), sem("dense_x"), sem("dense_st")
        dense_a_used, dense_rows_used, dense_ready = sem("dense_a_used"), sem("dense_rows_used"), sem("dense_ready")
        dense_step = sem("dense_step")

        adj_half = adj.rearrange("(t p) (h w) -> t h p w", p=P, h=2)
        adj_chunk = adj.rearrange("(g r p) (c w) -> g c p r w", r=RT, p=P, w=CH)
        x_tiles = x.rearrange("(t p) c -> p t c", p=P)
        x_groups = x.rearrange("(g r p) c -> g p r c", r=RT, p=P)
        x1_groups = x1_rows.rearrange("(g r p) c -> g p r c", r=RT, p=P)
        out_groups = [tab[1:N // PARTS + 1, :].rearrange("(g r p) c -> g p r c", r=RT, p=P) for tab in out_table]
        FT = TILES // 8
        FIN = TILES // FT
        fin_pooled = pooled.rearrange("(q f t p) c -> f q p t c", q=PARTS, t=FT, p=P)
        fin_x1 = x1_rows.rearrange("(f t p) c -> f p t c", t=FT, p=P)
        fin_out = out.rearrange("(f t p) c -> f p t c", t=FT, p=P)
        fin_in = [a_buf[:, 2 * b:2 * b + 2, :].rearrange("p n w -> p (n w)")[:, 0:PARTS * FT * C]
                  .rearrange("p (q w) -> p q w", q=PARTS) for b in range(2)]
        fin_m = h_rows.rearrange("p t c -> p (t c)")
        a_tile = [a_buf[:, b, 0:HALF] for b in range(NB)]
        a_grp = [a_buf[:, b, :].rearrange("p (r w) -> p r w", r=RT) for b in range(NB)]
        DJ = 16
        dense_tab = [tab[1:N // PARTS + 1, :].rearrange("(k j) c -> k (j c)", j=DJ) for tab in out_table]
        dense_adj = adj.rearrange("(t p) (c w) -> t c p w", p=P, w=CH)
        dense_x1 = x1_rows.rearrange("(t p) c -> t p c", p=P)
        dense_o = out.rearrange("(t p) c -> t p c", p=P)

        P1_LOADS, P2_LOADS = 2 * BLOCKS, 2 * BLOCKS + GROUPS * CHUNKS // NB
        P1_USED = 2 * TILES
        PER = CHUNKS // NB

        def store_final(sp, f):
            sp.wait_ge(fin_ready, f + 1)
            b = f % 2
            sp.dma_start(fin_out[f], fin_m[:, (6 + b) * FT * C:(7 + b) * FT * C]
                         .rearrange("p (t c) -> p t c", c=C)).then_inc(fin_stored[b], 16)

        def nest(eng, slots, emit):
            def level(k0):
                for k in range(k0, k0 + 4):
                    if k == 0:
                        emit(k)
                    elif k == k0:
                        emit(k)
                    else:
                        with eng.If(slots > k):
                            emit(k)
                if k0 + 4 < KQ:
                    with eng.If(slots > k0 + 4):
                        level(k0 + 4)
            level(0)

        block = ctx.enter_context(nc.Block())

        @block.sync
        def _(sp):
            def hold(s, value):
                sp.wait_ge(s, value)
                sp.sem_inc(sp_held, 1)

            sp.dma_start(x_in[:, 0:NB, :], x_tiles[:, 0:NB, :]).then_inc(x_first, 16)
            sp.dma_start(cols_in[0:2, :], times).then_inc(small_in, 16)
            sp.dma_start(cols_in[2:3, :], bias.rearrange("(o c) -> o c", o=1)).then_inc(small_in, 16)
            sp.dma_start(mass_in[:, :], mass.rearrange("(t p) -> t p", p=P)).then_inc(small_in, 16)
            sp.dma_start(ev0[:, :], evals0.rearrange("(o v) -> o v", o=1).broadcast_to([P, V0])).then_inc(small_in, 16)
            sp.dma_start(ev1[:, :], evals1.rearrange("(o v) -> o v", o=1).broadcast_to([P, V1])).then_inc(small_in, 16)
            sp.dma_start(w_sb[:, :], weight).then_inc(small_in, 16)
            for b in range(2):
                sp.dma_start(a_tile[b], adj_half[b, 0]).then_inc(a_loaded[b], 16)
            sp.dma_start(x_in[:, NB:, :], x_tiles[:, NB:, :]).then_inc(x_rest, 16)
            for b in range(2, NB):
                sp.dma_start(a_tile[b], adj_half[b, 0]).then_inc(a_loaded[b], 16)
            for h in range(2):
                lo = 1 if h == 0 else 0
                with sp.Fori(lo, BLOCKS) as b:
                    for j in range(NB):
                        hold(pe_used, (b + h * BLOCKS) * NB + j + 1)
                        if j < LT:
                            hold(dve_used, (b + h * BLOCKS) * LT + j + 1)
                        sp.dma_start(a_tile[j], adj_half[b * NB + j, h]).then_inc(a_loaded[j], 16)
            sp.wait_ge(dve_used, LT + 2 * BLOCKS * LT)
            with sp.Fori(0, GROUPS) as g:
                for c in range(CHUNKS):
                    if c < NB:
                        sp.wait_ge(pe_used, P1_USED + c + 1)
                    hold(turned, g * (CHUNKS * JT) + (c + 1) * JT)
                    hold(dve_chunk, g * CHUNKS + c + 1)
                    sp.dma_start(a_grp[c % NB], adj_chunk[g, c]).then_inc(a_loaded[c % NB], 16)
            sp.wait_ge(dve_chunk, NB + GROUPS * CHUNKS)
            with sp.Fori(0, GROUPS) as g:
                for c in range(CHUNKS):
                    hold(turned, (g + GROUPS) * (CHUNKS * JT) + (c + 1) * JT)
                    sp.dma_start(a_grp[c % NB], adj_chunk[g, c]).then_inc(a_loaded[c % NB], 16)
            sp.wait_ge(turned, (NB + 2 * GROUPS * CHUNKS) * JT)
            sp.wait_ge(mm_done, 2 * GROUPS * CHUNKS * JT)
            for b in range(2):
                sp.wait_ge(acc_out[b], 16 * PARTS * TILES // 2)
            for f in range(FIN):
                b = f % 2
                if f >= 2:
                    sp.wait_ge(fin_ready, f - 1)
                    sp.wait_ge(fin_stored[b], 16 * (f // 2))
                for q in range(PARTS):
                    sp.dma_start(fin_in[b][:, q, :].rearrange("p (t c) -> p t c", c=C),
                                 fin_pooled[f, q]).then_inc(fin_loaded[b], 16)
                sp.dma_start(y_buf[:, b * FT * C:(b + 1) * FT * C].rearrange("p (t c) -> p t c", c=C),
                             fin_x1[f]).then_inc(fin_loaded[b], 16)
                if f >= 1:
                    store_final(sp, f - 1)
            store_final(sp, FIN - 1)
            for b in range(2):
                sp.wait_ge(fin_stored[b], 16 * (FIN // 2))
            sp.wait_ge(flag_set, 1)
            flag = sp.value_load(flag_i[0:1, 0:1], min_val=0, max_val=1)

            with sp.If(flag > 0):
                with sp.Fori(0, TILES) as t:
                    for c in range(CHUNKS):
                        hold(dense_a_used, t * CHUNKS + c + 1)
                        sp.dma_start(a_buf[:, 0, 0:CH], dense_adj[t, c]).then_inc(dense_a, 16)
                        part, k0 = divmod(c * (CH // DJ), N // PARTS // DJ)
                        with sp.Fori(0, CH // DJ) as k:
                            hold(dense_rows_used, t * (N // DJ) + k + c * (CH // DJ) + 1)
                            sp.dma_start(a_buf[:, 1, 0:DJ * C],
                                         dense_tab[part][bass.ds(k + k0, 1), :].broadcast_to([P, DJ * C])
                                         ).then_inc(dense_out, 16)
                    sp.dma_start(x1_grp[:, 0, :], dense_x1[t]).then_inc(dense_x, 16)
                    hold(dense_ready, t + 1)
                    sp.dma_start(dense_o[t], x1_grp[:, 1, :]).then_inc(dense_st, 16)
                    hold(dense_st, t * 16 + 16)

        @block.gpsimd
        def _(pool):
            steps = Steps(pool_step, pool.wait_ge)

            def hold(s, value):
                pool.wait_ge(s, value)
                pool.sem_inc(pool_held, 1)

            steps.step(pool.memset(ident[:, :], 0.0))
            steps.step(pool.memset(tri[:, :], 0.0))
            pool.iota(iota_seg, [[1, SEG]], base=1, channel_multiplier=0, allow_small_or_imprecise_dtypes=True)
            pool.memset(half_pow[:, :], -0.5)
            pool.iota(seg_base.rearrange("p (q s k) -> p q s k", q=2, k=TOP), [[0, 2], [SEG, HSEGS // 2], [0, TOP]], base=0,
                      channel_multiplier=0, allow_small_or_imprecise_dtypes=True)
            steps.settle()
            steps.step(pool.affine_select(out=ident[:, :], in_=ident[:, :], compare_op=ALU.not_equal, fill=1.0, base=0,
                                          pattern=[[-1, P]], channel_multiplier=1))
            steps.step(pool.affine_select(out=tri[:, :], in_=tri[:, :], compare_op=ALU.is_ge, fill=1.0, base=0,
                                          pattern=[[-1, P]], channel_multiplier=1))
            pool.memset(ones[:, :], 1.0)
            pool.memset(lists[:, :, :, KQ:LIST], 0)
            pool.memset(grow[:, :, :], 0)
            pool.memset(none_row[:, :], -BIG)
            pool.iota(deg_iota[:, :, :], [[0, PARTS], [-1, DEG]], base=KQ, channel_multiplier=0,
                      allow_small_or_imprecise_dtypes=True)
            steps.step(pool.iota(row_iota[:, :], [[P, TILES]], base=0, channel_multiplier=1,
                                 allow_small_or_imprecise_dtypes=True))
            steps.settle()
            pool.sem_inc(consts, 1)
            for q in range(PARTS):
                pool.dma_start(out_table[q][0:1, :], none_row[:, :]).then_inc(none_stored, 16)
            pool.sem_inc(x1_free, 1)

            with pool.Fori(0, BLOCKS) as b:
                pool.wait_ge(var_ready, b + 1)
                pool.tensor_tensor(rstd[:, :], var[:, :], half_pow[:, :], ALU.pow).then_inc(rstd_ready, 1)
            with pool.Fori(0, GROUPS) as g:
                hold(xg_read, g + 1)
                pool.dma_start(x_grp[:, :, :], x_groups[g]).then_inc(xg_loaded, 16)
                pool.wait_ge(var_ready, g + BLOCKS + 1)
                pool.tensor_tensor(rstd[:, :], var[:, :], half_pow[:, :], ALU.pow).then_inc(rstd_ready, 1)
                hold(x1_ready, g + 1)
                pool.dma_start(x1_groups[g], x1_grp[:, :, :]).then_inc(x1_stored, 16)
                pool.wait_ge(x1_stored, g * 16 + 16)
                pool.sem_inc(x1_free, 1)

            for q in range(PARTS):
                with pool.Fori(0, TILES // 4) as t:
                    for s in range(4):
                        hold(scat_staged, t * 4 + q * TILES + s + 1)
                        pool.indirect_dma_start(sorted_lists, bass.IndirectOffsetOnAxis(ap=scat[:, s, RANK:RANK + 1], axis=0),
                                                scat[:, s, :], None).then_inc(scat_done[s], 16)
            for s in range(4):
                pool.wait_ge(scat_done[s], 16 * PARTS * TILES // 4)
            by_rank = sorted_lists.rearrange("(q t p) l -> q p t l", q=PARTS, p=P)
            for q in range(PARTS):
                pool.dma_start(sorted_s[:, q * TILES:(q + 1) * TILES, :], by_rank[q]).then_inc(lists_loaded, 16)
            pool.wait_ge(none_stored, 16 * PARTS)

            def gather(q, u, p):
                hold(glist_ready, u + 1)
                hold(acc_ready, u + 1)
                slots = pool.value_load(glist[0:1, p, DEGREE:DEGREE + 1], min_val=1, max_val=KQ)

                def fetch(k):
                    pool.indirect_dma_start(gathered_rows[:, p, k, :], None, out_table[q],
                                            bass.IndirectOffsetOnAxis(ap=glist[:, p, k:k + 1], axis=0)
                                            ).then_inc(rows_in[p], 16)
                nest(pool, slots, fetch)

            def scatter(u, p):
                hold(acc_ready, u + 3)
                pool.indirect_dma_start(pooled, bass.IndirectOffsetOnAxis(ap=grow[:, p, 0:1], axis=0),
                                        pool_acc[:, p, :], None).then_inc(acc_out[p], 16)

            for q in range(PARTS):
                pool.wait_ge(out_stored, 16 * OT * (q + 1))
                u0 = q * TILES
                gather(q, u0, 0)
                with pool.Fori(0, TILES // 2 - 1) as i:
                    gather(q, i * 2 + u0 + 1, 1)
                    scatter(i * 2 + u0, 0)
                    gather(q, i * 2 + u0 + 2, 0)
                    scatter(i * 2 + u0 + 1, 1)
                gather(q, u0 + TILES - 1, 1)
                scatter(u0 + TILES - 2, 0)
                scatter(u0 + TILES - 1, 1)

        @block.scalar
        def _(act):
            act.sem_inc(acc_saved, 1)
            act.wait_ge(cols_copied, 1)
            act.wait_ge(small_in, 16 * 6)
            act.activation(e0[:, :], ev0[:, :], ACT.Exp, scale=cols[:, 0:1])
            act.activation(e1[:, :], ev1[:, :], ACT.Exp, scale=cols[:, 1:2]).then_inc(exp_done, 1)
            for k in range(N // W):
                act.wait_ge(yt_turned, k + 1)
                act.activation(y_t[:, k * W:(k + 1) * W], ps[:, k % 4, :], ACT.Copy).then_inc(y_ready, 1)

            def group(G):
                for jt in range(CHUNKS * JT):
                    act.wait_ge(turned, G * (CHUNKS * JT) + NB * JT + jt + 1)
                    if jt >= 4:
                        act.wait_ge(mm_done, G * (CHUNKS * JT) + jt - 3)
                    act.activation(at_buf[:, jt % 4, :], ps[:, TP + jt % 4, :], ACT.Copy).then_inc(at_copied, 1)
                act.wait_ge(mm_done, (G + 1) * (CHUNKS * JT))
                act.activation(acc_s[:, :], ps[:, ACC, :], ACT.Copy).then_inc(acc_saved, 1)

            with act.Fori(0, GROUPS) as g:
                group(g)
            with act.Fori(0, PARTS) as q:
                with act.Fori(0, OT) as i:
                    g = act.snap(q * OT + i)
                    group(g + GROUPS)
                    act.wait_ge(product_done, g + 1)
                    act.activation(out_t[:, :], ps[:, OUTB, :], ACT.Relu, bias=cols[:, 2:3]).then_inc(out_t_ready, 1)
                    act.wait_ge(rows_turned, g + 1)
                    act.activation(out_rows[:, :, :], ps[:, ROWB, :].rearrange("p (r c) -> p r c", c=C),
                                   ACT.Copy).then_inc(rows_copied, 1)
                    act.wait_ge(rows_copied, g + 1)
                    act.sem_inc(act_held, 1)
                    for quarter in range(PARTS):
                        with act.If(q == quarter):
                            act.dma_start(out_groups[quarter][i], out_rows[:, :, :]).then_inc(out_stored, 16)
                    act.wait_ge(out_stored, g * 16 + 16)
                    act.sem_inc(act_held, 1)

        @block.tensor
        def _(pe):
            pe.sem_inc(pe_used, NB)
            pe.sem_inc(turned, NB * JT)
            pe.wait_ge(consts, 1)
            pe.wait_ge(small_in, 16 * 6)
            pe.transpose(ps[:, SMALL, 0:3], cols_in[:, :], ident[0:3, 0:3])
            pe.transpose(ps[:, SMALL, 4:4 + TILES], mass_in[:, :], ident[0:TILES, 0:TILES]).then_inc(cols_turned, 1)
            pe.wait_ge(cols_copied, 1)
            with pe.Fori(0, 2) as h:
                for b in range(BLOCKS):
                    pe.wait_ge(xm_ready, b + 1)
                    for j in range(NB):
                        t = b * NB + j
                        pe.wait_ge(a_loaded[j], h * (16 * BLOCKS) + 16 * (b + 1))
                        for k in range(BANKS):
                            if t == 0:
                                pe.wait_ge(bank_read, h * BANKS + k + 1)
                            mm = pe.matmul(ps[:, k, :], h_rows[:, t, :], a_tile[j][:, k * W:(k + 1) * W],
                                           start=(t == 0), stop=(t == TILES - 1))
                            if t == TILES - 1 and k < BANKS - 1:
                                mm.then_inc(half_done, 1)
                        mm.then_inc(pe_used, 1)
            for k in range(N // W):
                pe.wait_ge(bank_read, 3 * BANKS)
                if k >= 4:
                    pe.wait_ge(y_ready, k - 3)
                for i in range(4):
                    mm = pe.transpose(ps[:, k % 4, i * P:(i + 1) * P], y_t[:, k * W + i * P:k * W + (i + 1) * P],
                                      ident[:, :])
                mm.then_inc(yt_turned, 1)
            pe.wait_ge(y_ready, N // W)

            def group(G, loads, operand):
                n = CHUNKS * JT
                for jt in range(n + LAG):
                    if jt < n:
                        c = jt // JT
                        if jt % JT == 0:
                            pe.wait_ge(a_loaded[c % NB], loads + 16 * (c // NB + 1))
                        if jt >= 4:
                            pe.wait_ge(at_copied, G * n + jt - 3)
                        for r in range(RT):
                            mm = pe.transpose(ps[:, TP + jt % 4, r * P:(r + 1) * P],
                                              a_grp[c % NB][:, r, (jt % JT) * P:(jt % JT + 1) * P], ident[:, :])
                        mm.then_inc(turned, 1)
                    if jt >= LAG:
                        k = jt - LAG
                        pe.wait_ge(at_copied, G * n + k + 1)
                        if k == 0:
                            pe.wait_ge(acc_saved, G + 1)
                        pe.matmul(ps[:, ACC, :], operand[:, k, :], at_buf[:, k % 4, :],
                                  start=(k == 0), stop=(k == n - 1)).then_inc(mm_done, 1)

            y_rows = y_buf.rearrange("p (t c) -> p t c", c=C)
            with pe.Fori(0, GROUPS) as g:
                group(g, g * (16 * PER) + 16 * P1_LOADS, y_rows)
                pe.wait_ge(acc_saved, g + 2)
                pe.wait_ge(x_turned_read, g + 1)
                for r in range(RT):
                    mm = pe.transpose(ps[:, OUTB, r * P:(r + 1) * P], acc_s[:, r * P:(r + 1) * P], ident[:, :])
                mm.then_inc(x_turned, 1)
            pe.wait_ge(h1_ready, GROUPS)
            with pe.Fori(0, GROUPS) as g:
                group(g + GROUPS, g * (16 * PER) + 16 * P2_LOADS, h_rows)
                pe.wait_ge(acc_saved, g + GROUPS + 2)
                pe.matmul(ps[:, OUTB, :], w_sb[:, :], acc_s[:, :], start=True, stop=True).then_inc(product_done, 1)
                pe.wait_ge(out_t_ready, g + 1)
                for r in range(RT):
                    mm = pe.transpose(ps[:, ROWB, r * P:(r + 1) * P], out_t[:, r * P:(r + 1) * P], ident[:, :])
                mm.then_inc(rows_turned, 1)
                with pe.If(g < 1):
                    pe.wait_ge(counted, 1)
                    pe.matmul(ps[:, SMALL, 0:PARTS * DEG], ones[:, :], count_b[:, :], start=True, stop=True)
                    pe.matmul(ps[:, SMALL, 128:128 + PARTS * DEG], tri[:, :], count_b[:, :], start=True, stop=True)
                    pe.matmul(ps[:, SMALL, 256:257], ones[:, :], flag_b[:, 0:1], start=True, stop=True).then_inc(summed, 1)

        @block.vector
        def _(dve):
            steps = Steps(dve_step, None)

            def hold(s, value):
                dve.wait_ge(s, value)
                dve.sem_inc(dve_held, 1)
            steps.wait = hold

            dve.sem_inc(dve_used, LT)
            dve.sem_inc(dve_chunk, NB)
            dve.sem_inc(bank_read, BANKS)
            dve.sem_inc(x_turned_read, 1)
            dve.sem_inc(xg_read, 1)
            dve.sem_inc(acc_ready, 2)
            dve.wait_ge(cols_turned, 1)
            steps.step(dve.tensor_scalar(cols[:, 0:2], ps[:, SMALL, 0:2], -1.0, None, ALU.mult))
            steps.step(dve.tensor_copy(cols[:, 2:3], ps[:, SMALL, 2:3]))
            steps.step(dve.tensor_copy(mass_c[:, :], ps[:, SMALL, 4:4 + TILES]))
            steps.settle()
            dve.sem_inc(cols_copied, 1)

            def stats_of(st, src):
                for r in range(RT):
                    st.step(dve.bn_stats(stats[:, r, :], src(r)))
                st.settle()
                for r in range(RT):
                    st.step(dve.bn_aggr(mv[:, r, :], stats[:, r, :]))
                st.settle()
                dve.tensor_scalar(var[:, :], mv[:, :, 1], EPS, None, ALU.add).then_inc(var_ready, 1)
            STATS = 2 * RT

            def centred(st, src):
                for r in range(RT):
                    st.step(dve.tensor_scalar(xc[:, r, :], src(r), mv[:, r, 0:1], 0.0, ALU.subtract, ALU.max))
                st.settle()
            CENTRED = RT

            def prepare_stats(b):
                stats_of(steps, lambda r: x_in[:, b * NB + r, :])

            def prepare_rows(b):
                centred(steps, lambda r: x_in[:, b * NB + r, :])
                hold(rstd_ready, b + 1)
                for r in range(NB):
                    ins = dve.tensor_scalar(h_rows[:, b * NB + r, :], xc[:, r, :], rstd[:, r:r + 1],
                                            mass_c[:, bass.ds(b * NB + r, 1)], ALU.mult, ALU.mult)
                    steps.step(ins) if r < NB - 1 else ins.then_inc(xm_ready, 1)
            PREPARE = STATS + CENTRED + NB - 1

            def keys_of(src, k0, n, sig):
                ins = dve.scalar_tensor_tensor(out=key[:, k0:k0 + n, :], in0=src, scalar=0.0,
                                               in1=iota_seg[:, None, :].broadcast_to([P, n, SEG]),
                                               op0=ALU.not_equal, op1=ALU.mult)
                ins.then_inc(sig, 1)

            def narrow(it, h):
                flat = cand.rearrange("p t s k -> p t (s k)")
                base = seg_base[:, None, :].broadcast_to([P, LT, HSEGS * TOP])
                steps.step(dve.scalar_tensor_tensor(out=moved, in0=flat, scalar=0.0, in1=base,
                                                    op0=ALU.is_gt, op1=ALU.mult))
                steps.step(dve.tensor_reduce(ovf[:, bass.ds(it, LT), h], cand[:, :, :, TOP - 1], AX_X, ALU.max))
                steps.settle()
                steps.step(dve.tensor_tensor(keys0, moved, flat, ALU.add))
                steps.settle()
                ks = [keys0, keys1, keys2]
                for r in range(KQ // TOP):
                    for t in range(LT):
                        for q in range(2):
                            steps.step(dve.max(raw[:, t, q, r * TOP:(r + 1) * TOP], ks[r][:, t, q * QC:(q + 1) * QC]))
                    steps.settle()
                    if r < KQ // TOP - 1:
                        for t in range(LT):
                            for q in range(2):
                                steps.step(dve.match_replace(ks[r + 1][:, t, q * QC:(q + 1) * QC],
                                                             raw[:, t, q, r * TOP:(r + 1) * TOP],
                                                             ks[r][:, t, q * QC:(q + 1) * QC], 0.0))
                        steps.settle()
                flat_raw = raw.rearrange("p t q k -> p (t q) k")
                steps.step(dve.scalar_tensor_tensor(out=fill.rearrange("p t q k -> p (t q) k"), in0=flat_raw, scalar=0.0,
                                                    in1=flat_raw[:, :, 0:1].broadcast_to([P, LT * 2, KQ]),
                                                    op0=ALU.is_equal, op1=ALU.mult))
                steps.settle()
                steps.step(dve.tensor_tensor(lists[:, bass.ds(it, LT), bass.ds(h * 2, 2), 0:KQ], raw, fill, ALU.add))
            NARROW = 5 + 4 * (KQ // TOP) + 4 * (KQ // TOP - 1)

            def list_block(b, h, between):
                for j in range(LT):
                    hold(a_loaded[j], (b + h * BLOCKS) * 16 + 16)
                    src = a_tile[j].rearrange("p (s c) -> p s c", c=SEG)
                    k2 = HSEGS // 2
                    steps.step(dve.scalar_tensor_tensor(out=key[:, 0:k2, :], in0=src[:, 0:k2, :], scalar=0.0,
                                                        in1=iota_seg[:, None, :].broadcast_to([P, k2, SEG]),
                                                        op0=ALU.not_equal, op1=ALU.mult))
                    keys_of(src[:, k2:, :], k2, HSEGS - k2, dve_used)
                    hold(dve_used, (b + h * BLOCKS) * LT + LT + j + 1)
                    for s in range(HSEGS):
                        steps.step(dve.max(cand[:, j, s, :], key[:, s, :]))
                    steps.settle()
                    if j == 0:
                        between()
                narrow(b * NB, h)
            BLOCK = LT * (1 + HSEGS) + NARROW

            def save_half(h):
                for k in range(BANKS):
                    dve.wait_ge(half_done if k < BANKS - 1 else pe_used,
                                h * (BANKS - 1) + k + 1 if k < BANKS - 1 else NB + (h + 1) * TILES)
                    for v in range(W // V1):
                        v0 = (h * HALF + k * W) // V1 + v
                        ins = dve.scalar_tensor_tensor(out=y_t[:, v0 * V1:(v0 + 1) * V1], in0=e1[:, :],
                                                       scalar=e0[:, v0:v0 + 1], in1=ps[:, k, v * V1:(v + 1) * V1],
                                                       op0=ALU.mult, op1=ALU.mult)
                    ins.then_inc(bank_read, 1)

            dve.wait_ge(consts, 1)
            dve.wait_ge(x_first, 16)
            prepare_stats(0)
            prepare_rows(0)
            dve.wait_ge(x_rest, 16)
            with dve.Fori(0, BLOCKS - 1) as b:
                steps.enter(b, PREPARE + BLOCK)
                prepare_stats(b + 1)
                list_block(b, 0, lambda: prepare_rows(b + 1))
                steps.leave(BLOCKS - 1)
            list_block(BLOCKS - 1, 0, lambda: None)
            dve.wait_ge(exp_done, 1)
            save_half(0)
            with dve.Fori(0, BLOCKS) as b:
                steps.enter(b, BLOCK)
                list_block(b, 1, lambda: None)
                steps.leave(BLOCKS)
            save_half(1)

            def list_chunk(g, c):
                hold(a_loaded[c % NB], g * (16 * PER) + 16 * (P1_LOADS + c // NB + 1))
                n = LT * CSEGS
                k0 = (c % 2) * n
                keys_of(a_grp[c % NB][:, LT:, :].rearrange("p r (s c) -> p (r s) c", c=SEG), k0, n, dve_chunk)
                hold(dve_chunk, g * CHUNKS + NB + c + 1)
                s0 = (c % (CHUNKS // 2)) * CSEGS
                for t in range(LT):
                    for s in range(CSEGS):
                        steps.step(dve.max(cand[:, t, s0 + s, :], key[:, k0 + t * CSEGS + s, :]))
                if c % (CHUNKS // 2) == CHUNKS // 2 - 1:
                    steps.settle()
                    narrow(g * RT + LT, c // (CHUNKS // 2))
                steps.settle()

            def residual(g):
                hold(x_turned, g + 1)
                hold(xg_loaded, g * 16 + 16)
                hold(x1_free, g + 1)
                dve.tensor_tensor(x1_grp[:, :, :], ps[:, OUTB, :].rearrange("p (r c) -> p r c", c=C), x_grp[:, :, :],
                                  ALU.add).then_inc(x1_ready, 1)
                hold(x1_ready, g + 1)
                dve.sem_inc(x_turned_read, 1)
                dve.sem_inc(xg_read, 1)
                stats_of(steps, lambda r: x1_grp[:, r, :])
                centred(steps, lambda r: x1_grp[:, r, :])
                hold(rstd_ready, g + BLOCKS + 1)
                for r in range(RT):
                    ins = dve.tensor_scalar(h_rows[:, g * RT + r, :], xc[:, r, :], rstd[:, r:r + 1], None, ALU.mult)
                    steps.step(ins) if r < RT - 1 else ins.then_inc(h1_ready, 1)
            RESIDUAL = STATS + CENTRED + RT - 1

            with dve.Fori(0, GROUPS) as g:
                steps.enter(g, CHUNKS * LT * CSEGS + 2 * NARROW + RESIDUAL)
                for c in range(CHUNKS):
                    list_chunk(g, c)
                residual(g)
                steps.leave(GROUPS)

            steps.wait = dve.wait_ge
            steps.settle()
            dve.wait_ge(x1_free, 1 + GROUPS)
            dve.wait_ge(h1_ready, GROUPS)
            dv = differs.rearrange("p (t k) -> p t k", k=KQ - 1)
            for q in range(PARTS):
                lq = lists[:, :, q, :]
                steps.step(dve.tensor_tensor(dv, lq[:, :, 1:KQ], lq[:, :, 0:KQ - 1], ALU.not_equal))
                steps.settle()
                steps.step(dve.tensor_reduce(degree[:, q, :], dv, AX_X, ALU.add))
                steps.settle()
                steps.step(dve.scalar_tensor_tensor(out=degree[:, q, :], in0=lq[:, :, 0], scalar=0.0,
                                                    in1=degree[:, q, :], op0=ALU.is_gt, op1=ALU.add))
                steps.settle()
                steps.step(dve.tensor_tensor(
                    onehot[:, q * DEG:(q + 1) * DEG, :], degree[:, q, :][:, None, :].broadcast_to([P, DEG, TILES]),
                    deg_iota[:, q, :][:, :, None].broadcast_to([P, DEG, TILES]), ALU.is_equal))
            steps.settle()
            steps.step(dve.tensor_reduce(count[:, :], onehot, AX_X, ALU.add))
            steps.step(dve.tensor_reduce(flag_c[:, 0:1], ovf.rearrange("p t h -> p (t h)"), AX_X, ALU.max))
            steps.step(dve.tensor_reduce(flag_c[:, 1:2], degree.rearrange("p q t -> p (q t)"), AX_X, ALU.max))
            steps.settle()
            steps.step(dve.tensor_copy(count_b[:, :], count[:, :]))
            steps.step(dve.tensor_scalar(flag_c[:, 2:3], flag_c[:, 1:2], KQ - 0.5, None, ALU.is_gt))
            steps.settle()
            steps.step(dve.tensor_tensor(flag_c[:, 3:4], flag_c[:, 0:1], flag_c[:, 2:3], ALU.add))
            steps.settle()
            steps.step(dve.tensor_scalar(flag_b[:, 0:1], flag_c[:, 3:4], 0.0, None, ALU.is_gt))
            steps.settle()
            dve.sem_inc(counted, 1)
            for q in range(PARTS):
                steps.step(dve.tensor_scalar(lists[:, :, q, ROWID], row_iota[:, :], float(q * N), None, ALU.add))
                steps.step(dve.tensor_scalar(lists[:, :, q, DEGREE], degree[:, q, :], 1.0, None, ALU.max))
            steps.step(dve.tensor_copy(before, onehot))
            steps.settle()
            IN = 8
            b4 = before.rearrange("p d (o i) -> p d o i", i=IN)
            for i in range(1, IN):
                steps.step(dve.tensor_tensor(b4[:, :, :, i], b4[:, :, :, i], b4[:, :, :, i - 1], ALU.add))
                steps.settle()
            for o in range(1, TILES // IN):
                steps.step(dve.tensor_tensor(b4[:, :, o, IN - 1], b4[:, :, o, IN - 1], b4[:, :, o - 1, IN - 1], ALU.add))
                steps.settle()
            for o in range(1, TILES // IN):
                steps.step(dve.tensor_tensor(
                    b4[:, :, o, 0:IN - 1], b4[:, :, o, 0:IN - 1],
                    b4[:, :, o - 1, IN - 1][:, :, None].broadcast_to([P, PARTS * DEG, IN - 1]), ALU.add))
            steps.settle()
            dve.wait_ge(summed, 1)
            steps.step(dve.tensor_copy(offs[:, 0, :], ps[:, SMALL, 0:PARTS * DEG]))
            steps.step(dve.tensor_copy(offs[:, 2, :], ps[:, SMALL, 128:128 + PARTS * DEG]))
            steps.step(dve.tensor_scalar(flag_i[0:1, 0:1], ps[0:1, SMALL, 256:257], 0.0, None, ALU.is_gt))
            steps.settle()
            dve.sem_inc(flag_set, 1)
            ov = offs.rearrange("p n (q d) -> p n q d", d=DEG)
            for d in range(1, DEG):
                steps.step(dve.tensor_tensor(ov[:, 0, :, d], ov[:, 0, :, d], ov[:, 0, :, d - 1], ALU.add))
                steps.settle()
            steps.step(dve.memset(ov[:, 1, :, 0], 0.0))
            steps.step(dve.tensor_copy(ov[:, 1, :, 1:DEG], ov[:, 0, :, 0:DEG - 1]))
            steps.settle()
            steps.step(dve.tensor_tensor(offs[:, 1, :], offs[:, 1, :], offs[:, 2, :], ALU.add))
            steps.settle()
            rn = rank_n.rearrange("p (d t) -> p d t", t=TILES)
            for q in range(PARTS):
                oh = onehot[:, q * DEG:(q + 1) * DEG, :]
                steps.step(dve.tensor_tensor(
                    rn, before[:, q * DEG:(q + 1) * DEG, :],
                    offs[:, 1, q * DEG:(q + 1) * DEG][:, :, None].broadcast_to([P, DEG, TILES]), ALU.add))
                steps.settle()
                steps.step(dve.tensor_tensor(rn, rn, oh, ALU.mult))
                steps.settle()
                steps.step(dve.tensor_reduce(rank[:, q, :], rn.rearrange("p d t -> p t d"), AX_X, ALU.add))
                steps.settle()
                steps.step(dve.tensor_scalar(lists[:, :, q, RANK], rank[:, q, :], float(q * N - 1), None, ALU.add))
                steps.settle()
            for q in range(PARTS):
                with dve.Fori(0, TILES // 4) as t:
                    for s in range(4):
                        if q == 0:
                            with dve.If(t > 0):
                                hold(scat_done[s], t * 16)
                        else:
                            hold(scat_done[s], t * 16 + 4 * q * TILES)
                        dve.tensor_copy(scat[:, s, :], lists[:, t * 4 + s, q, :]).then_inc(scat_staged, 1)

            dve.wait_ge(lists_loaded, 16 * PARTS)
            rows_sum = [dve.alloc_register(f"rows_sum{p}") for p in range(2)]
            done_sum = dve.alloc_register("done_sum")
            for r in (*rows_sum, done_sum):
                dve.reg_mov(r, 0)

            def stage(u, p):
                dve.tensor_copy(glist[:, p, :], sorted_s[:, bass.ds(u, 1), :].rearrange("p u l -> p (u l)")
                                ).then_inc(glist_ready, 1)

            def reduce(u, pairs, p):
                hold(glist_ready, u + 1)
                slots = dve.value_load(glist[0:1, p, DEGREE:DEGREE + 1], min_val=1, max_val=KQ)
                dve.reg_add(rows_sum[p], rows_sum[p], slots)
                total = dve.snap(rows_sum[p])
                start = dve.snap(done_sum)
                hold(rows_in[p], total * 16)
                with dve.If(pairs > 0):
                    hold(acc_out[p], pairs * 16)
                dve.tensor_copy(grow[:, p, 0:1], glist[:, p, ROWID:ROWID + 1])

                def take(k):
                    if k == 0:
                        dve.tensor_copy(pool_acc[:, p, :], gathered_rows[:, p, 0, :]).then_inc(red_step, 1)
                    else:
                        hold(red_step, start + k)
                        dve.tensor_tensor(pool_acc[:, p, :], pool_acc[:, p, :], gathered_rows[:, p, k, :],
                                          ALU.max).then_inc(red_step, 1)
                nest(dve, slots, take)
                dve.reg_add(done_sum, done_sum, slots)
                end = dve.snap(done_sum)
                hold(red_step, end)
                dve.sem_inc(acc_ready, 1)

            HT = TILES // 2
            with dve.Fori(0, PARTS) as q:
                stage(q * TILES, 0)
                stage(q * TILES + 1, 1)
                with dve.Fori(0, HT - 1) as i:
                    for p in range(2):
                        reduce(q * TILES + i * 2 + p, q * HT + i, p)
                        stage(q * TILES + i * 2 + p + 2, p)
                for p in range(2):
                    reduce(q * TILES + TILES - 2 + p, q * HT + HT - 1, p)

            fin = Steps(fin_step, dve.wait_ge)
            for f in range(FIN):
                b = f % 2
                L = FT * C
                dve.wait_ge(fin_loaded[b], 16 * (PARTS + 1) * (f // 2 + 1))
                m = [fin_m[:, (3 * b + i) * L:(3 * b + i + 1) * L] for i in range(3)]
                o = fin_m[:, (6 + b) * L:(7 + b) * L]
                fin.step(dve.tensor_tensor(m[0], fin_in[b][:, 0, :], fin_in[b][:, 1, :], ALU.max))
                fin.step(dve.tensor_tensor(m[1], fin_in[b][:, 2, :], fin_in[b][:, 3, :], ALU.max))
                fin.settle()
                fin.step(dve.tensor_tensor(m[2], m[0], m[1], ALU.max))
                fin.settle()
                if f >= 2:
                    dve.wait_ge(fin_stored[b], 16 * (f // 2))
                dve.tensor_tensor(o, m[2], y_buf[:, b * L:(b + 1) * L], ALU.add).then_inc(fin_ready, 1)

            flag = dve.value_load(flag_i[0:1, 0:1], min_val=0, max_val=1)
            dve.wait_ge(fin_ready, FIN)
            with dve.If(flag > 0):
                limit, unset = a_buf[:, 2, 0:CH], a_buf[:, 2, CH:2 * CH]
                capped = a_buf[:, 3, 0:DJ * C].rearrange("p (j c) -> p j c", c=C)
                rows = a_buf[:, 1, 0:DJ * C].rearrange("p (j c) -> p j c", c=C)
                best, most = x1_grp[:, 2, :], x1_grp[:, 3, :]
                KJ = CH // DJ
                dense = Steps(dense_step, hold)
                dve.sem_inc(dense_a_used, 1)
                dve.sem_inc(dense_rows_used, 1)
                with dve.Fori(0, TILES) as t:
                    PER_T = 2 + CHUNKS * (3 + KJ * 3)
                    base_t = t * PER_T
                    dve.memset(most, -BIG).then_inc(dense_step, 1)
                    with dve.Fori(0, CHUNKS) as c:
                        base_c = base_t + c * (3 + KJ * 3) + 1
                        hold(dense_step, base_c)
                        hold(dense_a, (t * CHUNKS + c) * 16 + 16)
                        dve.tensor_scalar(limit, a_buf[:, 0, 0:CH], 0.0, BIG, ALU.not_equal, ALU.mult
                                          ).then_inc(dense_step, 1)
                        dve.tensor_scalar(unset, a_buf[:, 0, 0:CH], 0.0, -BIG, ALU.is_equal, ALU.mult
                                          ).then_inc(dense_step, 1)
                        hold(dense_step, base_c + 2)
                        dve.sem_inc(dense_a_used, 1)
                        dve.tensor_tensor(limit, limit, unset, ALU.add).then_inc(dense_step, 1)
                        hold(dense_step, base_c + 3)
                        with dve.Fori(0, KJ) as k:
                            base_k = base_c + k * 3 + 3
                            hold(dense_out, ((t * CHUNKS + c) * KJ + k) * 16 + 16)
                            dve.tensor_tensor(capped, rows,
                                              limit[:, bass.ds(k * DJ, DJ)][:, :, None].broadcast_to([P, DJ, C]),
                                              ALU.min).then_inc(dense_step, 1)
                            hold(dense_step, base_k + 1)
                            dve.sem_inc(dense_rows_used, 1)
                            dve.tensor_reduce(best, capped.rearrange("p j c -> p c j"), AX_X, ALU.max
                                              ).then_inc(dense_step, 1)
                            hold(dense_step, base_k + 2)
                            dve.tensor_tensor(most, most, best, ALU.max).then_inc(dense_step, 1)
                            hold(dense_step, base_k + 3)
                    hold(dense_x, t * 16 + 16)
                    dve.tensor_tensor(x1_grp[:, 1, :], x1_grp[:, 0, :], most, ALU.add).then_inc(dense_step, 1)
                    hold(dense_step, base_t + PER_T)
                    dve.sem_inc(dense_ready, 1)
                    hold(dense_st, t * 16 + 16)


_INS = ["x", "adj", "L0_gnn_mass", "L0_gnn_evals0", "L0_gnn_evals1", "L0_gnn_diffusion_time", "L1_gnn_weight",
        "L1_gnn_bias"]


def kernel(**inputs):
    import numpy as _np
    import concourse.bacc as _bacc
    from concourse import mybir as _mybir
    from concourse.bass_utils import run_bass_kernel_spmd as _run

    nc = _bacc.Bacc("TRN2", target_bir_lowering=False, num_devices=1)
    arrays, args = {}, []
    for name in _INS:
        a = _np.ascontiguousarray(inputs[name])
        arrays[f"in_{name}_dram"] = a
        args.append(nc.dram_tensor(f"in_{name}_dram", a.shape, _mybir.dt.from_np(a.dtype), kind="ExternalInput").ap())
    shape = inputs["x"].shape
    args.append(nc.dram_tensor("out_0_dram", shape, _mybir.dt.float32, kind="ExternalOutput").ap())
    diffusion_and_pool_kernel(nc, *args)
    r = _run(nc, [arrays], core_ids=[0])
    return r.results[0]["out_0_dram"]
```

```python
from contextlib import ExitStack

import numpy as np

import concourse.bass as bass
from concourse import mybir

P = 128
W = 512
SEG = 256
TOP = 8
PARTS = 4
KQ = 24
ROWID, DEGREE, RANK, LIST = 24, 25, 26, 32
NB = 4
RT = 4
CH = 1024
SR = 8
GR = 4
LAG = 2
BIG = float(np.finfo(np.float32).max)
EPS = 1e-5

ALU = mybir.AluOpType
ACT = mybir.ActivationFunctionType
AX_X = mybir.AxisListType.X
F32 = mybir.dt.float32
BF16 = mybir.dt.bfloat16
U16 = mybir.dt.uint16
U32 = mybir.dt.uint32
I32 = mybir.dt.int32


class Steps:

    def __init__(self, sem, wait):
        self.sem, self.wait, self.base, self.n = sem, wait, 0, 0

    def step(self, ins):
        ins.then_inc(self.sem, 1)
        self.n += 1

    def settle(self):
        self.wait(self.sem, self.base + self.n)

    def enter(self, i, per):
        self.outer, self.per = self.base + self.n, per
        self.base, self.n = i * per + self.outer, 0

    def leave(self, rounds):
        assert self.n == self.per, (self.n, self.per)
        self.base, self.n = self.outer + rounds * self.per, 0


def diffusion_and_pool_kernel(nc, x, adj, mass, evals0, evals1, times, weight, bias, out):
    N, C = x.shape
    V0, V1 = evals0.shape[0], evals1.shape[0]
    assert C == P and V1 == P and V0 * V1 == N and adj.shape == (N, N)
    TILES = N // P
    HALF = N // 2
    BANKS = HALF // W
    HSEGS = HALF // SEG
    QC = HSEGS * TOP // 2
    BLOCKS = TILES // NB
    GROUPS = TILES // RT
    CHUNKS = N // CH
    JT = CH // P
    CSEGS = CH // SEG
    LT = NB // 2
    assert RT == NB == 2 * LT and CHUNKS % NB == 0 and BANKS <= 8
    DEG = KQ + 1
    OT = GROUPS // PARTS

    with ExitStack() as ctx:
        def sb(name, shape, dt=F32):
            return ctx.enter_context(nc.sbuf_tensor(name, shape, dt))

        def sem(name):
            return ctx.enter_context(nc.semaphore(name))

        def sems(name, n):
            return [sem(f"{name}{i}") for i in range(n)]

        out_table = [nc.dram_tensor(f"out_table{q}", [N // PARTS + 1, C], F32).ap() for q in range(PARTS)]
        sorted_lists = nc.dram_tensor("sorted_lists", [PARTS * N, LIST], U16).ap()
        pooled = nc.dram_tensor("pooled", [PARTS * N, C], F32).ap()
        x1_rows = nc.dram_tensor("x1_rows", [N, C], F32).ap()

        a_buf = sb("a_buf", [P, NB, RT * CH])
        h_rows = sb("h_rows", [P, TILES, C])
        SORTED = PARTS * TILES * LIST // 2
        y_all = sb("y_all", [P, max(N, SORTED + KQ * C)])
        y_buf = y_all[:, 0:N]
        lists_all = sb("lists_all", [P, max(2 * SORTED, 2 * KQ * C)], U16)
        lists = lists_all[:, 0:2 * SORTED].rearrange("p (t q l) -> p t q l", q=PARTS, l=LIST)
        at_buf = sb("at_buf", [P, 4, W])
        acc_s = sb("acc_s", [P, W])
        out_t = sb("out_t", [P, W])
        out_rows = sb("out_rows", [P, RT, C])
        work = sb("work", [P, max(3 * RT * C, DEG * TILES)])
        x_grp, x1_grp, xc = (work[:, i * RT * C:(i + 1) * RT * C].rearrange("p (r c) -> p r c", c=C) for i in range(3))
        z_buf = sb("z_buf", [P, 26 * 1024 // 4])
        ident = sb("ident", [P, P])
        w_sb = sb("w_sb", [P, C])
        cols_in = sb("cols_in", [3, P])
        cols = sb("cols", [P, 4])
        mass_in = sb("mass_in", [TILES, P])
        mass_c = sb("mass_c", [P, TILES])
        ev0 = sb("ev0_s", [P, V0])
        ev1 = sb("ev1_s", [P, V1])
        e0 = sb("e0", [P, V0])
        e1 = sb("e1", [P, V1])
        stats = sb("stats", [P, RT, 6])
        mv = sb("mv", [P, RT, 2])
        var = sb("var", [P, RT])
        rstd = sb("rstd", [P, RT])
        shift = sb("shift", [P, RT])
        half_pow = sb("half_pow", [P, RT])
        ovf = sb("ovf", [P, TILES, 2])
        tri = sb("tri", [P, P], BF16)
        ones = sb("ones", [P, P], BF16)
        flag_c = sb("flag_c", [P, 4])
        flag_b = sb("flag_b", [P, 2], BF16)
        flag_i = sb("flag_i", [1, 2], I32)

        x_in = y_buf.rearrange("p (t c) -> p t c", c=C)
        spare_rows = y_all[:, SORTED:]
        y_t = y_buf
        sorted_s = y_all[:, 0:SORTED].bitcast(U16).rearrange("p (u l) -> p u l", l=LIST)

        def carve(at, shape, dt):
            n = int(np.prod(shape)) * (2 if dt in (BF16, U16) else 4)
            v = z_buf[:, at // 4:(at + n) // 4]
            if dt != F32:
                v = v.bitcast(dt)
            names = "abcd"[:len(shape)]
            if len(shape) > 1:
                v = v.rearrange(f"p ({' '.join(names)}) -> p {' '.join(names)}", **dict(zip(names, shape)))
            return v, at + n

        key, z = carve(0, (LT * CH * 2 // SEG, SEG), BF16)
        iota_seg, z = carve(z, (SEG,), F32)
        seg_base, z = carve(z, (HSEGS * TOP,), F32)
        cand, z = carve(z, (LT, HSEGS, TOP), BF16)
        moved, z = carve(z, (LT, HSEGS * TOP), F32)
        keys0, z = carve(z, (LT, HSEGS * TOP), F32)
        keys1, z = carve(z, (LT, HSEGS * TOP), F32)
        keys2, z = carve(z, (LT, HSEGS * TOP), F32)
        raw, z = carve(z, (LT, 2, KQ), F32)
        fill, z = carve(z, (LT, 2, KQ), F32)
        assert z <= 26 * 1024
        onehot, z = carve(0, (PARTS * DEG, TILES), BF16)
        before, z = carve(z, (PARTS * DEG, TILES), BF16)
        in_z, _ = carve(0, (2, KQ, C), F32)
        in_lists = lists_all.bitcast(F32)
        gathered_rows = [in_z[:, 0], in_z[:, 1]] + [
            v[:, 0:KQ * C].rearrange("p (k c) -> p k c", c=C) for v in (spare_rows, in_lists)]
        rank_n = work[:, 0:DEG * TILES]
        differs = rank_n[:, 0:TILES * (KQ - 1)]
        degree = sb("degree", [P, PARTS, TILES])
        deg_iota = sb("deg_iota", [P, PARTS, DEG])
        row_iota = sb("row_iota", [P, TILES])
        count = sb("count", [P, PARTS * DEG])
        count_b = sb("count_b", [P, PARTS * DEG], BF16)
        offs = sb("offs", [P, 3, PARTS * DEG])
        rank = sb("rank", [P, PARTS, TILES])
        scat = sb("scat", [P, SR, LIST], U16)
        scat_to = sb("scat_to", [P, SR, 1], U32)
        glist = sb("glist", [P, GR, LIST], U32)
        grow = sb("grow", [P, GR, 1], U32)
        pool_acc = sb("pool_acc", [P, GR, C])
        none_row = sb("none_row", [1, C])

        ps = ctx.enter_context(nc.psum_tensor("ps", [P, 8, W], F32))
        TP, ACC, OUTB, ROWB, SMALL = 0, 4, 5, 6, 7

        consts = sem("consts")
        small_in = sem("small_in")
        x_first, x_rest = sem("x_first"), sem("x_rest")
        cols_turned, cols_copied, exp_done = sem("cols_turned"), sem("cols_copied"), sem("exp_done")
        a_loaded = sems("a_loaded", NB)
        pe_used, dve_used, dve_chunk = sem("pe_used"), sem("dve_used"), sem("dve_chunk")
        var_ready, rstd_ready = sem("var_ready"), sem("rstd_ready")
        shift_ready, relu_done, xm_ready = sem("shift_ready"), sem("relu_done"), sem("xm_ready")
        half_done, bank_read = sem("half_done"), sem("bank_read")
        yt_turned, y_ready = sem("yt_turned"), sem("y_ready")
        turned, at_copied, mm_done = sem("turned"), sem("at_copied"), sem("mm_done")
        acc_done, acc_saved = sem("acc_done"), sem("acc_saved")
        x_turned, x_turned_read = sem("x_turned"), sem("x_turned_read")
        xg_loaded, xg_read = sem("xg_loaded"), sem("xg_read")
        x1_ready, x1_stored, x1_free = sem("x1_ready"), sem("x1_stored"), sem("x1_free")
        h1_ready = sem("h1_ready")
        product_done, out_t_ready, rows_turned = sem("product_done"), sem("out_t_ready"), sem("rows_turned")
        rows_copied, out_stored = sem("rows_copied"), sem("out_stored")
        listed = sem("listed")
        counted, summed, ranked, flag_in, flag_sum, flag_set = (
            sem("counted"), sem("summed"), sem("ranked"), sem("flag_in"), sem("flag_sum"), sem("flag_set"))
        scat_staged, scat_done = sem("scat_staged"), sems("scat_done", SR)
        lists_loaded = sems("lists_loaded", PARTS)
        glist_ready, acc_ready = sem("glist_ready"), sem("acc_ready")
        rows_in, acc_out = sems("rows_in", GR), sems("acc_out", GR)
        none_stored = sem("none_stored")
        pool_held, dve_held, act_held, sp_held = sem("pool_held"), sem("dve_held"), sem("act_held"), sem("sp_held")
        dve_step, pool_step, red_step, fin_step, merge_step = (
            sem("dve_step"), sem("pool_step"), sem("red_step"), sem("fin_step"), sem("merge_step"))
        x1_back, merge_read, merge_loaded = sem("x1_back"), sem("merge_read"), sems("merge_loaded", 2)
        last_loaded, fin_stored, fin_ready = sems("last_loaded", TILES // (TILES // 8)), sem("fin_stored"), sem("fin_ready")
        dense_a, dense_out, dense_x, dense_st = sem("dense_a"), sem("dense_out"), sem("dense_x"), sem("dense_st")
        dense_a_used, dense_rows_used, dense_ready = sem("dense_a_used"), sem("dense_rows_used"), sem("dense_ready")
        dense_step = sem("dense_step")

        adj_half = adj.rearrange("(t p) (h w) -> t h p w", p=P, h=2)
        adj_chunk = adj.rearrange("(g r p) (c w) -> g c p r w", r=RT, p=P, w=CH)
        x_tiles = x.rearrange("(t p) c -> p t c", p=P)
        x_groups = x.rearrange("(g r p) c -> g p r c", r=RT, p=P)
        x1_groups = x1_rows.rearrange("(g r p) c -> g p r c", r=RT, p=P)
        out_groups = [tab[1:N // PARTS + 1, :].rearrange("(g r p) c -> g p r c", r=RT, p=P) for tab in out_table]
        FT = TILES // 8
        FIN = TILES // FT
        MT = GR
        L = MT * C
        pooled_mt = pooled.rearrange("(q f t p) c -> f q p t c", q=PARTS, t=MT, p=P)
        pooled_last = pooled.rearrange("(q f t p) c -> q f p t c", q=PARTS, t=FT, p=P)[PARTS - 1]
        x1_ft = x1_rows.rearrange("(f t p) c -> f p t c", t=FT, p=P)
        out_ft = out.rearrange("(f t p) c -> f p t c", t=FT, p=P)
        def rows_of(v):
            return v.rearrange("p (t c) -> p t c", c=C)
        a_flat = a_buf.rearrange("p n w -> p (n w)")
        x1_all, last_all = rows_of(a_flat[:, 0:N]), rows_of(a_flat[:, N:2 * N])
        merge_in = [a_flat[:, N + b * 3 * L:N + (b + 1) * 3 * L].rearrange("p (q w) -> p q w", q=3) for b in range(2)]
        merged = h_rows.rearrange("p t c -> p (t c)")
        merge_tmp = at_buf.rearrange("p n w -> p (n w)")[:, 0:L]
        a_tile = [a_buf[:, b, 0:HALF] for b in range(NB)]
        a_grp = [a_buf[:, b, :].rearrange("p (r w) -> p r w", r=RT) for b in range(NB)]
        DJ = 16
        dense_tab = [tab[1:N // PARTS + 1, :].rearrange("(k j) c -> k (j c)", j=DJ) for tab in out_table]
        dense_adj = adj.rearrange("(t p) (c w) -> t c p w", p=P, w=CH)
        dense_x1 = x1_rows.rearrange("(t p) c -> t p c", p=P)
        dense_o = out.rearrange("(t p) c -> t p c", p=P)

        P1_LOADS, P2_LOADS = 2 * BLOCKS, 2 * BLOCKS + GROUPS * CHUNKS // NB
        P1_USED = 2 * TILES
        PER = CHUNKS // NB

        def nest(eng, slots, emit):
            def level(k0):
                for k in range(k0, k0 + 4):
                    if k == 0:
                        emit(k)
                    elif k == k0:
                        emit(k)
                    else:
                        with eng.If(slots > k):
                            emit(k)
                if k0 + 4 < KQ:
                    with eng.If(slots > k0 + 4):
                        level(k0 + 4)
            level(0)

        block = ctx.enter_context(nc.Block())

        @block.sync
        def _(sp):
            def hold(s, value):
                sp.wait_ge(s, value)
                sp.sem_inc(sp_held, 1)

            sp.dma_start(x_in[:, 0:NB, :], x_tiles[:, 0:NB, :]).then_inc(x_first, 16)
            sp.dma_start(cols_in[0:2, :], times).then_inc(small_in, 16)
            sp.dma_start(cols_in[2:3, :], bias.rearrange("(o c) -> o c", o=1)).then_inc(small_in, 16)
            sp.dma_start(mass_in[:, :], mass.rearrange("(t p) -> t p", p=P)).then_inc(small_in, 16)
            sp.dma_start(ev0[:, :], evals0.rearrange("(o v) -> o v", o=1).broadcast_to([P, V0])).then_inc(small_in, 16)
            sp.dma_start(ev1[:, :], evals1.rearrange("(o v) -> o v", o=1).broadcast_to([P, V1])).then_inc(small_in, 16)
            sp.dma_start(w_sb[:, :], weight).then_inc(small_in, 16)
            for b in range(2):
                sp.dma_start(a_tile[b], adj_half[b, 0]).then_inc(a_loaded[b], 16)
            sp.dma_start(x_in[:, NB:, :], x_tiles[:, NB:, :]).then_inc(x_rest, 16)
            for b in range(2, NB):
                sp.dma_start(a_tile[b], adj_half[b, 0]).then_inc(a_loaded[b], 16)
            for h in range(2):
                lo = 1 if h == 0 else 0
                with sp.Fori(lo, BLOCKS) as b:
                    for j in range(NB):
                        hold(pe_used, (b + h * BLOCKS) * NB + j + 1)
                        if j < LT:
                            hold(dve_used, (b + h * BLOCKS) * LT + j + 1)
                        sp.dma_start(a_tile[j], adj_half[b * NB + j, h]).then_inc(a_loaded[j], 16)
            sp.wait_ge(dve_used, LT + 2 * BLOCKS * LT)
            with sp.Fori(0, GROUPS) as g:
                for c in range(CHUNKS):
                    if c < NB:
                        sp.wait_ge(pe_used, P1_USED + c + 1)
                    hold(turned, g * (CHUNKS * JT) + (c + 1) * JT)
                    hold(dve_chunk, g * CHUNKS + c + 1)
                    sp.dma_start(a_grp[c % NB], adj_chunk[g, c]).then_inc(a_loaded[c % NB], 16)
            sp.wait_ge(dve_chunk, NB + GROUPS * CHUNKS)
            with sp.Fori(0, GROUPS) as g:
                for c in range(CHUNKS):
                    hold(turned, (g + GROUPS) * (CHUNKS * JT) + (c + 1) * JT)
                    sp.dma_start(a_grp[c % NB], adj_chunk[g, c]).then_inc(a_loaded[c % NB], 16)
            sp.wait_ge(turned, (NB + 2 * GROUPS * CHUNKS) * JT)
            sp.wait_ge(mm_done, 2 * GROUPS * CHUNKS * JT)
            for f in range(FIN):
                sp.dma_start(x1_all[:, f * FT:(f + 1) * FT, :], x1_ft[f]).then_inc(x1_back, 16)
            for p in range(GR):
                sp.wait_ge(acc_out[p], 16 * (PARTS - 1) * TILES // GR)
            with sp.Fori(0, TILES // MT // 2) as i:
                for b in range(2):
                    hold(merge_read, i * 2 + b + 1)
                    for q in range(PARTS - 1):
                        sp.dma_start(rows_of(merge_in[b][:, q, :]), pooled_mt[i * 2 + b, q]).then_inc(merge_loaded[b], 16)
            sp.wait_ge(merge_read, 2 + TILES // MT)
            for p in range(GR):
                sp.wait_ge(acc_out[p], 16 * PARTS * TILES // GR)
            for f in range(FIN):
                sp.dma_start(last_all[:, f * FT:(f + 1) * FT, :], pooled_last[f]).then_inc(last_loaded[f], 16)
            for f in range(FIN):
                sp.wait_ge(fin_ready, f + 1)
                sp.dma_start(out_ft[f], last_all[:, f * FT:(f + 1) * FT, :]).then_inc(fin_stored, 16)
            sp.wait_ge(fin_stored, 16 * FIN)
            sp.wait_ge(flag_set, 1)
            flag = sp.value_load(flag_i[0:1, 0:1], min_val=0, max_val=1)

            with sp.If(flag > 0):
                with sp.Fori(0, TILES) as t:
                    for c in range(CHUNKS):
                        hold(dense_a_used, t * CHUNKS + c + 1)
                        sp.dma_start(a_buf[:, 0, 0:CH], dense_adj[t, c]).then_inc(dense_a, 16)
                        part, k0 = divmod(c * (CH // DJ), N // PARTS // DJ)
                        with sp.Fori(0, CH // DJ) as k:
                            hold(dense_rows_used, t * (N // DJ) + k + c * (CH // DJ) + 1)
                            sp.dma_start(a_buf[:, 1, 0:DJ * C],
                                         dense_tab[part][bass.ds(k + k0, 1), :].broadcast_to([P, DJ * C])
                                         ).then_inc(dense_out, 16)
                    sp.dma_start(x1_grp[:, 0, :], dense_x1[t]).then_inc(dense_x, 16)
                    hold(dense_ready, t + 1)
                    sp.dma_start(dense_o[t], x1_grp[:, 1, :]).then_inc(dense_st, 16)
                    hold(dense_st, t * 16 + 16)

        @block.gpsimd
        def _(pool):
            steps = Steps(pool_step, pool.wait_ge)

            def hold(s, value):
                pool.wait_ge(s, value)
                pool.sem_inc(pool_held, 1)

            steps.step(pool.memset(ident[:, :], 0.0))
            steps.step(pool.memset(tri[:, :], 0.0))
            pool.iota(iota_seg, [[1, SEG]], base=1, channel_multiplier=0, allow_small_or_imprecise_dtypes=True)
            pool.memset(half_pow[:, :], -0.5)
            pool.iota(seg_base.rearrange("p (q s k) -> p q s k", q=2, k=TOP), [[0, 2], [SEG, HSEGS // 2], [0, TOP]], base=0,
                      channel_multiplier=0, allow_small_or_imprecise_dtypes=True)
            steps.settle()
            steps.step(pool.affine_select(out=ident[:, :], in_=ident[:, :], compare_op=ALU.not_equal, fill=1.0, base=0,
                                          pattern=[[-1, P]], channel_multiplier=1))
            steps.step(pool.affine_select(out=tri[:, :], in_=tri[:, :], compare_op=ALU.is_ge, fill=1.0, base=0,
                                          pattern=[[-1, P]], channel_multiplier=1))
            pool.memset(ones[:, :], 1.0)
            pool.memset(lists[:, :, :, KQ:LIST], 0)
            pool.memset(grow[:, :, :], 0)
            pool.memset(none_row[:, :], -BIG)
            pool.iota(deg_iota[:, :, :], [[0, PARTS], [-1, DEG]], base=KQ, channel_multiplier=0,
                      allow_small_or_imprecise_dtypes=True)
            steps.step(pool.iota(row_iota[:, :], [[P, TILES]], base=0, channel_multiplier=1,
                                 allow_small_or_imprecise_dtypes=True))
            steps.settle()
            pool.sem_inc(consts, 1)
            for q in range(PARTS):
                pool.dma_start(out_table[q][0:1, :], none_row[:, :]).then_inc(none_stored, 16)
            pool.sem_inc(x1_free, 1)

            with pool.Fori(0, BLOCKS) as b:
                pool.wait_ge(var_ready, b + 1)
                pool.tensor_tensor(rstd[:, :], var[:, :], half_pow[:, :], ALU.pow).then_inc(rstd_ready, 1)
            with pool.Fori(0, GROUPS) as g:
                hold(xg_read, g + 1)
                pool.dma_start(x_grp[:, :, :], x_groups[g]).then_inc(xg_loaded, 16)
                pool.wait_ge(var_ready, g + BLOCKS + 1)
                pool.tensor_tensor(rstd[:, :], var[:, :], half_pow[:, :], ALU.pow).then_inc(rstd_ready, 1)
                hold(x1_ready, g + 1)
                pool.dma_start(x1_groups[g], x1_grp[:, :, :]).then_inc(x1_stored, 16)
                pool.wait_ge(x1_stored, g * 16 + 16)
                pool.sem_inc(x1_free, 1)

            for q in range(PARTS):
                with pool.Fori(0, TILES // SR) as t:
                    for r in range(SR):
                        hold(scat_staged, t * SR + q * TILES + r + 1)
                        pool.indirect_dma_start(sorted_lists, bass.IndirectOffsetOnAxis(ap=scat_to[:, r, 0:1], axis=0),
                                                scat[:, r, :], None).then_inc(scat_done[r], 16)
            for r in range(SR):
                pool.wait_ge(scat_done[r], 16 * PARTS * TILES // SR)
            by_rank = sorted_lists.rearrange("(q t p) l -> q p t l", q=PARTS, p=P)
            for q in range(PARTS):
                pool.dma_start(sorted_s[:, q * TILES:(q + 1) * TILES, :], by_rank[q]).then_inc(lists_loaded[q], 16)
            pool.wait_ge(none_stored, 16 * PARTS)

            def gather(q, u, p):
                hold(glist_ready, u + 1)
                hold(acc_ready, u + 1)
                slots = pool.value_load(glist[0:1, p, DEGREE:DEGREE + 1], min_val=1, max_val=KQ)

                def fetch(k):
                    pool.indirect_dma_start(gathered_rows[p][:, k, :], None, out_table[q],
                                            bass.IndirectOffsetOnAxis(ap=glist[:, p, k:k + 1], axis=0)
                                            ).then_inc(rows_in[p], 16)
                nest(pool, slots, fetch)

            def scatter(u, p):
                hold(acc_ready, u + GR - 1)
                pool.indirect_dma_start(pooled, bass.IndirectOffsetOnAxis(ap=grow[:, (p - 2) % GR, 0:1], axis=0),
                                        pool_acc[:, (p - 2) % GR, :], None).then_inc(acc_out[(p - 2) % GR], 16)

            for q in range(PARTS):
                pool.wait_ge(out_stored, 16 * OT * (q + 1))
                with pool.Fori(0, TILES // GR) as i:
                    for p in range(GR):
                        u = i * GR + (q * TILES + p)
                        gather(q, u, p)
                        if q == 0 and p < 2:
                            with pool.If(i > 0):
                                scatter(u, p)
                        else:
                            scatter(u, p)
            for p in range(2):
                scatter(PARTS * TILES + p, p)

        @block.scalar
        def _(act):
            act.sem_inc(acc_saved, 1)
            act.wait_ge(cols_copied, 1)
            act.wait_ge(small_in, 16 * 6)
            act.activation(e0[:, :], ev0[:, :], ACT.Exp, scale=cols[:, 0:1])
            act.activation(e1[:, :], ev1[:, :], ACT.Exp, scale=cols[:, 1:2]).then_inc(exp_done, 1)
            with act.Fori(0, BLOCKS) as b:
                act.wait_ge(shift_ready, b + 1)
                for r in range(NB):
                    ins = act.activation(xc[:, r, :], x_in[:, b * NB + r, :], ACT.Relu, bias=shift[:, r:r + 1],
                                         scale=rstd[:, r:r + 1])
                ins.then_inc(relu_done, 1)
                act.wait_ge(relu_done, b + 1)
                for r in range(NB):
                    ins = act.activation(h_rows[:, b * NB + r, :], xc[:, r, :], ACT.Copy,
                                         scale=mass_c[:, bass.ds(b * NB + r, 1)])
                ins.then_inc(xm_ready, 1)
            for k in range(N // W):
                act.wait_ge(yt_turned, k + 1)
                act.activation(y_t[:, k * W:(k + 1) * W], ps[:, k % 4, :], ACT.Copy).then_inc(y_ready, 1)

            def group(G):
                for jt in range(CHUNKS * JT):
                    act.wait_ge(turned, G * (CHUNKS * JT) + NB * JT + jt + 1)
                    if jt >= 4:
                        act.wait_ge(mm_done, G * (CHUNKS * JT) + jt - 3)
                    act.activation(at_buf[:, jt % 4, :], ps[:, TP + jt % 4, :], ACT.Copy).then_inc(at_copied, 1)
                act.wait_ge(mm_done, (G + 1) * (CHUNKS * JT))
                act.activation(acc_s[:, :], ps[:, ACC, :], ACT.Copy).then_inc(acc_saved, 1)

            with act.Fori(0, GROUPS) as g:
                group(g)
            with act.Fori(0, PARTS) as q:
                with act.Fori(0, OT) as i:
                    g = act.snap(q * OT + i)
                    group(g + GROUPS)
                    act.wait_ge(product_done, g + 1)
                    act.activation(out_t[:, :], ps[:, OUTB, :], ACT.Relu, bias=cols[:, 2:3]).then_inc(out_t_ready, 1)
                    act.wait_ge(rows_turned, g + 1)
                    act.activation(out_rows[:, :, :], ps[:, ROWB, :].rearrange("p (r c) -> p r c", c=C),
                                   ACT.Copy).then_inc(rows_copied, 1)
                    act.wait_ge(rows_copied, g + 1)
                    act.sem_inc(act_held, 1)
                    for quarter in range(PARTS):
                        with act.If(q == quarter):
                            act.dma_start(out_groups[quarter][i], out_rows[:, :, :]).then_inc(out_stored, 16)
                    act.wait_ge(out_stored, g * 16 + 16)
                    act.sem_inc(act_held, 1)

        @block.tensor
        def _(pe):
            pe.sem_inc(pe_used, NB)
            pe.sem_inc(turned, NB * JT)
            pe.wait_ge(consts, 1)
            pe.wait_ge(small_in, 16 * 6)
            pe.transpose(ps[:, SMALL, 0:3], cols_in[:, :], ident[0:3, 0:3])
            pe.transpose(ps[:, SMALL, 4:4 + TILES], mass_in[:, :], ident[0:TILES, 0:TILES]).then_inc(cols_turned, 1)
            pe.wait_ge(cols_copied, 1)
            with pe.Fori(0, 2) as h:
                for b in range(BLOCKS):
                    pe.wait_ge(xm_ready, b + 1)
                    for j in range(NB):
                        t = b * NB + j
                        pe.wait_ge(a_loaded[j], h * (16 * BLOCKS) + 16 * (b + 1))
                        for k in range(BANKS):
                            if t == 0:
                                pe.wait_ge(bank_read, h * BANKS + k + 1)
                            mm = pe.matmul(ps[:, k, :], h_rows[:, t, :], a_tile[j][:, k * W:(k + 1) * W],
                                           start=(t == 0), stop=(t == TILES - 1))
                            if t == TILES - 1 and k < BANKS - 1:
                                mm.then_inc(half_done, 1)
                        mm.then_inc(pe_used, 1)
            for k in range(N // W):
                pe.wait_ge(bank_read, 3 * BANKS)
                if k >= 4:
                    pe.wait_ge(y_ready, k - 3)
                for i in range(4):
                    mm = pe.transpose(ps[:, k % 4, i * P:(i + 1) * P], y_t[:, k * W + i * P:k * W + (i + 1) * P],
                                      ident[:, :])
                mm.then_inc(yt_turned, 1)
            pe.wait_ge(y_ready, N // W)

            def group(G, loads, operand):
                n = CHUNKS * JT
                for jt in range(n + LAG):
                    if jt < n:
                        c = jt // JT
                        if jt % JT == 0:
                            pe.wait_ge(a_loaded[c % NB], loads + 16 * (c // NB + 1))
                        if jt >= 4:
                            pe.wait_ge(at_copied, G * n + jt - 3)
                        for r in range(RT):
                            mm = pe.transpose(ps[:, TP + jt % 4, r * P:(r + 1) * P],
                                              a_grp[c % NB][:, r, (jt % JT) * P:(jt % JT + 1) * P], ident[:, :])
                        mm.then_inc(turned, 1)
                    if jt >= LAG:
                        k = jt - LAG
                        pe.wait_ge(at_copied, G * n + k + 1)
                        if k == 0:
                            pe.wait_ge(acc_saved, G + 1)
                        pe.matmul(ps[:, ACC, :], operand[:, k, :], at_buf[:, k % 4, :],
                                  start=(k == 0), stop=(k == n - 1)).then_inc(mm_done, 1)

            y_rows = y_buf.rearrange("p (t c) -> p t c", c=C)
            with pe.Fori(0, GROUPS) as g:
                group(g, g * (16 * PER) + 16 * P1_LOADS, y_rows)
                pe.wait_ge(acc_saved, g + 2)
                pe.wait_ge(x_turned_read, g + 1)
                for r in range(RT):
                    mm = pe.transpose(ps[:, OUTB, r * P:(r + 1) * P], acc_s[:, r * P:(r + 1) * P], ident[:, :])
                mm.then_inc(x_turned, 1)
            pe.wait_ge(h1_ready, GROUPS)
            with pe.Fori(0, GROUPS) as g:
                group(g + GROUPS, g * (16 * PER) + 16 * P2_LOADS, h_rows)
                pe.wait_ge(acc_saved, g + GROUPS + 2)
                pe.matmul(ps[:, OUTB, :], w_sb[:, :], acc_s[:, :], start=True, stop=True).then_inc(product_done, 1)
                pe.wait_ge(out_t_ready, g + 1)
                for r in range(RT):
                    mm = pe.transpose(ps[:, ROWB, r * P:(r + 1) * P], out_t[:, r * P:(r + 1) * P], ident[:, :])
                mm.then_inc(rows_turned, 1)
                with pe.If(g < 1):
                    pe.wait_ge(counted, 1)
                    pe.matmul(ps[:, SMALL, 0:PARTS * DEG], ones[:, :], count_b[:, :], start=True, stop=True)
                    pe.matmul(ps[:, SMALL, 128:128 + PARTS * DEG], tri[:, :], count_b[:, :], start=True, stop=True)
                    pe.matmul(ps[:, SMALL, 256:257], ones[:, :], flag_b[:, 0:1], start=True, stop=True).then_inc(summed, 1)

        @block.vector
        def _(dve):
            steps = Steps(dve_step, None)

            def hold(s, value):
                dve.wait_ge(s, value)
                dve.sem_inc(dve_held, 1)
            steps.wait = hold

            dve.sem_inc(dve_used, LT)
            dve.sem_inc(dve_chunk, NB)
            dve.sem_inc(bank_read, BANKS)
            dve.sem_inc(x_turned_read, 1)
            dve.sem_inc(xg_read, 1)
            dve.sem_inc(acc_ready, GR)
            dve.sem_inc(merge_read, 2)
            dve.wait_ge(cols_turned, 1)
            steps.step(dve.tensor_scalar(cols[:, 0:2], ps[:, SMALL, 0:2], -1.0, None, ALU.mult))
            steps.step(dve.tensor_copy(cols[:, 2:3], ps[:, SMALL, 2:3]))
            steps.step(dve.tensor_copy(mass_c[:, :], ps[:, SMALL, 4:4 + TILES]))
            steps.settle()
            dve.sem_inc(cols_copied, 1)

            def stats_of(st, src):
                for r in range(RT):
                    st.step(dve.bn_stats(stats[:, r, :], src(r)))
                st.settle()
                for r in range(RT):
                    st.step(dve.bn_aggr(mv[:, r, :], stats[:, r, :]))
                st.settle()
                dve.tensor_scalar(var[:, :], mv[:, :, 1], EPS, None, ALU.add).then_inc(var_ready, 1)
            STATS = 2 * RT

            def centred(st, src):
                for r in range(RT):
                    st.step(dve.tensor_scalar(xc[:, r, :], src(r), mv[:, r, 0:1], 0.0, ALU.subtract, ALU.max))
                st.settle()
            CENTRED = RT

            def prepare_stats(b):
                stats_of(steps, lambda r: x_in[:, b * NB + r, :])

            def prepare_shift(b):
                hold(rstd_ready, b + 1)
                dve.scalar_tensor_tensor(out=shift[:, :], in0=mv[:, :, 0], scalar=-1.0, in1=rstd[:, :],
                                         op0=ALU.mult, op1=ALU.mult).then_inc(shift_ready, 1)
            PREPARE = STATS

            def keys_of(src, k0, n, sig):
                ins = dve.scalar_tensor_tensor(out=key[:, k0:k0 + n, :], in0=src, scalar=0.0,
                                               in1=iota_seg[:, None, :].broadcast_to([P, n, SEG]),
                                               op0=ALU.not_equal, op1=ALU.mult)
                ins.then_inc(sig, 1)

            def narrow(it, h):
                flat = cand.rearrange("p t s k -> p t (s k)")
                base = seg_base[:, None, :].broadcast_to([P, LT, HSEGS * TOP])
                steps.step(dve.scalar_tensor_tensor(out=moved, in0=flat, scalar=0.0, in1=base,
                                                    op0=ALU.is_gt, op1=ALU.mult))
                steps.step(dve.tensor_reduce(ovf[:, bass.ds(it, LT), h], cand[:, :, :, TOP - 1], AX_X, ALU.max))
                steps.settle()
                steps.step(dve.tensor_tensor(keys0, moved, flat, ALU.add))
                steps.settle()
                ks = [keys0, keys1, keys2]
                for r in range(KQ // TOP):
                    for t in range(LT):
                        for q in range(2):
                            steps.step(dve.max(raw[:, t, q, r * TOP:(r + 1) * TOP], ks[r][:, t, q * QC:(q + 1) * QC]))
                    steps.settle()
                    if r < KQ // TOP - 1:
                        for t in range(LT):
                            for q in range(2):
                                steps.step(dve.match_replace(ks[r + 1][:, t, q * QC:(q + 1) * QC],
                                                             raw[:, t, q, r * TOP:(r + 1) * TOP],
                                                             ks[r][:, t, q * QC:(q + 1) * QC], 0.0))
                        steps.settle()
                flat_raw = raw.rearrange("p t q k -> p (t q) k")
                steps.step(dve.scalar_tensor_tensor(out=fill.rearrange("p t q k -> p (t q) k"), in0=flat_raw, scalar=0.0,
                                                    in1=flat_raw[:, :, 0:1].broadcast_to([P, LT * 2, KQ]),
                                                    op0=ALU.is_equal, op1=ALU.mult))
                steps.settle()
                steps.step(dve.tensor_tensor(lists[:, bass.ds(it, LT), bass.ds(h * 2, 2), 0:KQ], raw, fill, ALU.add))
            NARROW = 5 + 4 * (KQ // TOP) + 4 * (KQ // TOP - 1)

            def list_block(b, h, between=lambda: None, before_narrow=lambda: None):
                for j in range(LT):
                    hold(a_loaded[j], (b + h * BLOCKS) * 16 + 16)
                    src = a_tile[j].rearrange("p (s c) -> p s c", c=SEG)
                    k2 = HSEGS // 2
                    steps.step(dve.scalar_tensor_tensor(out=key[:, 0:k2, :], in0=src[:, 0:k2, :], scalar=0.0,
                                                        in1=iota_seg[:, None, :].broadcast_to([P, k2, SEG]),
                                                        op0=ALU.not_equal, op1=ALU.mult))
                    keys_of(src[:, k2:, :], k2, HSEGS - k2, dve_used)
                    hold(dve_used, (b + h * BLOCKS) * LT + LT + j + 1)
                    for s in range(HSEGS):
                        steps.step(dve.max(cand[:, j, s, :], key[:, s, :]))
                    steps.settle()
                    if j == 0:
                        between()
                before_narrow()
                narrow(b * NB, h)
            BLOCK = LT * (1 + HSEGS) + NARROW

            def save_half(h):
                for k in range(BANKS):
                    dve.wait_ge(half_done if k < BANKS - 1 else pe_used,
                                h * (BANKS - 1) + k + 1 if k < BANKS - 1 else NB + (h + 1) * TILES)
                    for v in range(W // V1):
                        v0 = (h * HALF + k * W) // V1 + v
                        ins = dve.scalar_tensor_tensor(out=y_t[:, v0 * V1:(v0 + 1) * V1], in0=e1[:, :],
                                                       scalar=e0[:, v0:v0 + 1], in1=ps[:, k, v * V1:(v + 1) * V1],
                                                       op0=ALU.mult, op1=ALU.mult)
                    ins.then_inc(bank_read, 1)

            dve.wait_ge(consts, 1)
            dve.wait_ge(x_first, 16)
            prepare_stats(0)
            prepare_shift(0)
            dve.wait_ge(x_rest, 16)
            with dve.Fori(0, BLOCKS - 1) as b:
                steps.enter(b, PREPARE + BLOCK)
                hold(xm_ready, b + 1)
                prepare_stats(b + 1)
                list_block(b, 0, lambda: prepare_shift(b + 1))
                steps.leave(BLOCKS - 1)
            dve.wait_ge(exp_done, 1)
            list_block(BLOCKS - 1, 0, before_narrow=lambda: save_half(0))
            with dve.Fori(0, BLOCKS - 1) as b:
                steps.enter(b, BLOCK)
                list_block(b, 1)
                steps.leave(BLOCKS - 1)
            list_block(BLOCKS - 1, 1, before_narrow=lambda: save_half(1))

            def list_chunk(g, c):
                hold(a_loaded[c % NB], g * (16 * PER) + 16 * (P1_LOADS + c // NB + 1))
                n = LT * CSEGS
                k0 = (c % 2) * n
                keys_of(a_grp[c % NB][:, LT:, :].rearrange("p r (s c) -> p (r s) c", c=SEG), k0, n, dve_chunk)
                hold(dve_chunk, g * CHUNKS + NB + c + 1)
                s0 = (c % (CHUNKS // 2)) * CSEGS
                for t in range(LT):
                    for s in range(CSEGS):
                        steps.step(dve.max(cand[:, t, s0 + s, :], key[:, k0 + t * CSEGS + s, :]))
                if c % (CHUNKS // 2) == CHUNKS // 2 - 1:
                    steps.settle()
                    narrow(g * RT + LT, c // (CHUNKS // 2))
                steps.settle()

            def residual(g):
                hold(x_turned, g + 1)
                hold(xg_loaded, g * 16 + 16)
                hold(x1_free, g + 1)
                dve.tensor_tensor(x1_grp[:, :, :], ps[:, OUTB, :].rearrange("p (r c) -> p r c", c=C), x_grp[:, :, :],
                                  ALU.add).then_inc(x1_ready, 1)
                hold(x1_ready, g + 1)
                dve.sem_inc(x_turned_read, 1)
                dve.sem_inc(xg_read, 1)
                stats_of(steps, lambda r: x1_grp[:, r, :])
                centred(steps, lambda r: x1_grp[:, r, :])
                hold(rstd_ready, g + BLOCKS + 1)
                for r in range(RT):
                    ins = dve.tensor_scalar(h_rows[:, g * RT + r, :], xc[:, r, :], rstd[:, r:r + 1], None, ALU.mult)
                    steps.step(ins) if r < RT - 1 else ins.then_inc(h1_ready, 1)
            RESIDUAL = STATS + CENTRED + RT - 1

            with dve.Fori(0, GROUPS) as g:
                steps.enter(g, CHUNKS * LT * CSEGS + 2 * NARROW + RESIDUAL)
                for c in range(CHUNKS):
                    list_chunk(g, c)
                residual(g)
                steps.leave(GROUPS)

            steps.wait = dve.wait_ge
            steps.settle()
            dve.wait_ge(x1_free, 1 + GROUPS)
            dve.wait_ge(h1_ready, GROUPS)
            dv = differs.rearrange("p (t k) -> p t k", k=KQ - 1)
            for q in range(PARTS):
                lq = lists[:, :, q, :]
                steps.step(dve.tensor_tensor(dv, lq[:, :, 1:KQ], lq[:, :, 0:KQ - 1], ALU.is_lt))
                steps.settle()
                steps.step(dve.tensor_reduce(degree[:, q, :], dv, AX_X, ALU.add))
                steps.settle()
                steps.step(dve.scalar_tensor_tensor(out=degree[:, q, :], in0=lq[:, :, 0], scalar=0.0,
                                                    in1=degree[:, q, :], op0=ALU.is_gt, op1=ALU.add))
                steps.settle()
                steps.step(dve.tensor_tensor(
                    onehot[:, q * DEG:(q + 1) * DEG, :], degree[:, q, :][:, None, :].broadcast_to([P, DEG, TILES]),
                    deg_iota[:, q, :][:, :, None].broadcast_to([P, DEG, TILES]), ALU.is_equal))
            steps.settle()
            steps.step(dve.tensor_reduce(count[:, :], onehot, AX_X, ALU.add))
            steps.step(dve.tensor_reduce(flag_c[:, 0:1], ovf.rearrange("p t h -> p (t h)"), AX_X, ALU.max))
            steps.step(dve.tensor_reduce(flag_c[:, 1:2], degree.rearrange("p q t -> p (q t)"), AX_X, ALU.max))
            steps.settle()
            steps.step(dve.tensor_copy(count_b[:, :], count[:, :]))
            steps.step(dve.tensor_scalar(flag_c[:, 2:3], flag_c[:, 1:2], KQ - 0.5, None, ALU.is_gt))
            steps.settle()
            steps.step(dve.tensor_tensor(flag_c[:, 3:4], flag_c[:, 0:1], flag_c[:, 2:3], ALU.add))
            steps.settle()
            steps.step(dve.tensor_scalar(flag_b[:, 0:1], flag_c[:, 3:4], 0.0, None, ALU.is_gt))
            steps.settle()
            dve.sem_inc(counted, 1)
            for q in range(PARTS):
                steps.step(dve.tensor_scalar(lists[:, :, q, ROWID], row_iota[:, :], float(q * N), None, ALU.add))
                steps.step(dve.tensor_scalar(lists[:, :, q, DEGREE], degree[:, q, :], 1.0, None, ALU.max))
            steps.step(dve.tensor_copy(before, onehot))
            steps.settle()
            IN = 8
            b4 = before.rearrange("p d (o i) -> p d o i", i=IN)
            for i in range(1, IN):
                steps.step(dve.tensor_tensor(b4[:, :, :, i], b4[:, :, :, i], b4[:, :, :, i - 1], ALU.add))
                steps.settle()
            for o in range(1, TILES // IN):
                steps.step(dve.tensor_tensor(b4[:, :, o, IN - 1], b4[:, :, o, IN - 1], b4[:, :, o - 1, IN - 1], ALU.add))
                steps.settle()
            for o in range(1, TILES // IN):
                steps.step(dve.tensor_tensor(
                    b4[:, :, o, 0:IN - 1], b4[:, :, o, 0:IN - 1],
                    b4[:, :, o - 1, IN - 1][:, :, None].broadcast_to([P, PARTS * DEG, IN - 1]), ALU.add))
            steps.settle()
            dve.wait_ge(summed, 1)
            steps.step(dve.tensor_copy(offs[:, 0, :], ps[:, SMALL, 0:PARTS * DEG]))
            steps.step(dve.tensor_copy(offs[:, 2, :], ps[:, SMALL, 128:128 + PARTS * DEG]))
            steps.step(dve.tensor_scalar(flag_i[0:1, 0:1], ps[0:1, SMALL, 256:257], 0.0, None, ALU.is_gt))
            steps.settle()
            dve.sem_inc(flag_set, 1)
            ov = offs.rearrange("p n (q d) -> p n q d", d=DEG)
            for d in range(1, DEG):
                steps.step(dve.tensor_tensor(ov[:, 0, :, d], ov[:, 0, :, d], ov[:, 0, :, d - 1], ALU.add))
                steps.settle()
            steps.step(dve.memset(ov[:, 1, :, 0], 0.0))
            steps.step(dve.tensor_copy(ov[:, 1, :, 1:DEG], ov[:, 0, :, 0:DEG - 1]))
            steps.settle()
            steps.step(dve.tensor_tensor(offs[:, 1, :], offs[:, 1, :], offs[:, 2, :], ALU.add))
            steps.settle()
            rn = rank_n.rearrange("p (d t) -> p d t", t=TILES)
            for q in range(PARTS):
                oh = onehot[:, q * DEG:(q + 1) * DEG, :]
                steps.step(dve.tensor_tensor(
                    rn, before[:, q * DEG:(q + 1) * DEG, :],
                    offs[:, 1, q * DEG:(q + 1) * DEG][:, :, None].broadcast_to([P, DEG, TILES]), ALU.add))
                steps.settle()
                steps.step(dve.tensor_tensor(rn, rn, oh, ALU.mult))
                steps.settle()
                steps.step(dve.tensor_reduce(rank[:, q, :], rn.rearrange("p d t -> p t d"), AX_X, ALU.add))
                steps.settle()
                steps.step(dve.tensor_scalar(lists[:, :, q, RANK], rank[:, q, :], float(q * N - 1), None, ALU.add))
                steps.settle()
            for q in range(PARTS):
                with dve.Fori(0, TILES // SR) as t:
                    for r in range(SR):
                        if q == 0:
                            with dve.If(t > 0):
                                hold(scat_done[r], t * 16)
                        else:
                            hold(scat_done[r], t * 16 + 16 * q * TILES // SR)
                        dve.tensor_copy(scat[:, r, :], lists[:, t * SR + r, q, :])
                        dve.tensor_copy(scat_to[:, r, :], lists[:, t * SR + r, q, RANK:RANK + 1]).then_inc(scat_staged, 1)

            rows_sum = [dve.alloc_register(f"rows_sum{p}") for p in range(GR)]
            done_sum = dve.alloc_register("done_sum")
            for r in (*rows_sum, done_sum):
                dve.reg_mov(r, 0)

            def stage(u, p):
                dve.tensor_copy(glist[:, p, :], sorted_s[:, bass.ds(u, 1), :].rearrange("p u l -> p (u l)")
                                ).then_inc(glist_ready, 1)

            def reduce(u, round_, p):
                hold(glist_ready, u + 1)
                slots = dve.value_load(glist[0:1, p, DEGREE:DEGREE + 1], min_val=1, max_val=KQ)
                dve.reg_add(rows_sum[p], rows_sum[p], slots)
                total = dve.snap(rows_sum[p])
                start = dve.snap(done_sum)
                hold(rows_in[p], total * 16)
                if isinstance(round_, int):
                    dve.wait_ge(acc_out[p], round_ * 16)
                else:
                    with dve.If(round_ > 0):
                        hold(acc_out[p], round_ * 16)
                dve.tensor_copy(grow[:, p, :], glist[:, p, ROWID:ROWID + 1])

                def take(k):
                    if k == 0:
                        dve.tensor_copy(pool_acc[:, p, :], gathered_rows[p][:, 0, :]).then_inc(red_step, 1)
                    else:
                        hold(red_step, start + k)
                        dve.tensor_tensor(pool_acc[:, p, :], pool_acc[:, p, :], gathered_rows[p][:, k, :],
                                          ALU.max).then_inc(red_step, 1)
                nest(dve, slots, take)
                dve.reg_add(done_sum, done_sum, slots)
                end = dve.snap(done_sum)
                hold(red_step, end)
                dve.sem_inc(acc_ready, 1)

            def merge(i):
                for b in range(2):
                    hold(merge_loaded[b], i * (16 * 3) + 16 * 3)
                    m = merged[:, bass.ds((i * 2 + b) * L, L)]
                    dve.tensor_tensor(merge_tmp, merge_in[b][:, 0, :], merge_in[b][:, 1, :], ALU.max).then_inc(merge_step, 1)
                    hold(merge_step, i * 4 + b * 2 + 1)
                    dve.tensor_tensor(m, merge_tmp, merge_in[b][:, 2, :], ALU.max).then_inc(merge_step, 1)
                    hold(merge_step, i * 4 + b * 2 + 2)
                    dve.sem_inc(merge_read, 1)

            QT = TILES // GR
            dve.wait_ge(lists_loaded[0], 16)
            for p in range(GR):
                stage(p, p)
            def tiles(q, i):
                for p in range(GR):
                    u = i * GR + (q * TILES + p)
                    reduce(u, i + q * QT, p)
                    stage(u + GR, p)

            for q in range(PARTS - 1):
                dve.wait_ge(lists_loaded[q + 1], 16)
                with dve.Fori(0, QT) as i:
                    tiles(q, i)
            with dve.Fori(0, QT // 2) as i:
                tiles(PARTS - 1, i)
                merge(i)
            with dve.Fori(QT // 2, QT - 1) as i:
                tiles(PARTS - 1, i)
            for p in range(GR):
                reduce((PARTS - 1) * TILES + TILES - GR + p, PARTS * QT - 1, p)

            fin = Steps(fin_step, dve.wait_ge)
            dve.wait_ge(x1_back, 16 * FIN)
            for f in range(FIN):
                rows = slice(f * FT, (f + 1) * FT)
                dve.wait_ge(last_loaded[f], 16)
                fin.step(dve.tensor_tensor(h_rows[:, rows, :], h_rows[:, rows, :], last_all[:, rows, :], ALU.max))
                fin.settle()
                dve.tensor_tensor(last_all[:, rows, :], h_rows[:, rows, :], x1_all[:, rows, :], ALU.add).then_inc(fin_ready, 1)

            flag = dve.value_load(flag_i[0:1, 0:1], min_val=0, max_val=1)
            dve.wait_ge(fin_stored, 16 * FIN)
            with dve.If(flag > 0):
                limit, unset = a_buf[:, 2, 0:CH], a_buf[:, 2, CH:2 * CH]
                capped = a_buf[:, 3, 0:DJ * C].rearrange("p (j c) -> p j c", c=C)
                rows = a_buf[:, 1, 0:DJ * C].rearrange("p (j c) -> p j c", c=C)
                best, most = x1_grp[:, 2, :], x1_grp[:, 3, :]
                KJ = CH // DJ
                dense = Steps(dense_step, hold)
                dve.sem_inc(dense_a_used, 1)
                dve.sem_inc(dense_rows_used, 1)
                with dve.Fori(0, TILES) as t:
                    PER_T = 2 + CHUNKS * (3 + KJ * 3)
                    base_t = t * PER_T
                    dve.memset(most, -BIG).then_inc(dense_step, 1)
                    with dve.Fori(0, CHUNKS) as c:
                        base_c = base_t + c * (3 + KJ * 3) + 1
                        hold(dense_step, base_c)
                        hold(dense_a, (t * CHUNKS + c) * 16 + 16)
                        dve.tensor_scalar(limit, a_buf[:, 0, 0:CH], 0.0, BIG, ALU.not_equal, ALU.mult
                                          ).then_inc(dense_step, 1)
                        dve.tensor_scalar(unset, a_buf[:, 0, 0:CH], 0.0, -BIG, ALU.is_equal, ALU.mult
                                          ).then_inc(dense_step, 1)
                        hold(dense_step, base_c + 2)
                        dve.sem_inc(dense_a_used, 1)
                        dve.tensor_tensor(limit, limit, unset, ALU.add).then_inc(dense_step, 1)
                        hold(dense_step, base_c + 3)
                        with dve.Fori(0, KJ) as k:
                            base_k = base_c + k * 3 + 3
                            hold(dense_out, ((t * CHUNKS + c) * KJ + k) * 16 + 16)
                            dve.tensor_tensor(capped, rows,
                                              limit[:, bass.ds(k * DJ, DJ)][:, :, None].broadcast_to([P, DJ, C]),
                                              ALU.min).then_inc(dense_step, 1)
                            hold(dense_step, base_k + 1)
                            dve.sem_inc(dense_rows_used, 1)
                            dve.tensor_reduce(best, capped.rearrange("p j c -> p c j"), AX_X, ALU.max
                                              ).then_inc(dense_step, 1)
                            hold(dense_step, base_k + 2)
                            dve.tensor_tensor(most, most, best, ALU.max).then_inc(dense_step, 1)
                            hold(dense_step, base_k + 3)
                    hold(dense_x, t * 16 + 16)
                    dve.tensor_tensor(x1_grp[:, 1, :], x1_grp[:, 0, :], most, ALU.add).then_inc(dense_step, 1)
                    hold(dense_step, base_t + PER_T)
                    dve.sem_inc(dense_ready, 1)
                    hold(dense_st, t * 16 + 16)


_INS = ["x", "adj", "L0_gnn_mass", "L0_gnn_evals0", "L0_gnn_evals1", "L0_gnn_diffusion_time", "L1_gnn_weight",
        "L1_gnn_bias"]


def kernel(**inputs):
    import numpy as _np
    import concourse.bacc as _bacc
    from concourse import mybir as _mybir
    from concourse.bass_utils import run_bass_kernel_spmd as _run

    nc = _bacc.Bacc("TRN2", target_bir_lowering=False, num_devices=1)
    arrays, args = {}, []
    for name in _INS:
        a = _np.ascontiguousarray(inputs[name])
        arrays[f"in_{name}_dram"] = a
        args.append(nc.dram_tensor(f"in_{name}_dram", a.shape, _mybir.dt.from_np(a.dtype), kind="ExternalInput").ap())
    shape = inputs["x"].shape
    args.append(nc.dram_tensor("out_0_dram", shape, _mybir.dt.float32, kind="ExternalOutput").ap())
    diffusion_and_pool_kernel(nc, *args)
    r = _run(nc, [arrays], core_ids=[0])
    return r.results[0]["out_0_dram"]
```
